# Optimizing a Trainium2 kernel written in Bass

```python
import numpy as np
import jax
import jax.numpy as jnp

def _softmax(x, axis=-1):
    return jax.nn.softmax(x, axis=axis)

def _gelu(x):
    return jax.nn.gelu(x, approximate=True)

def _silu(x):
    return jax.nn.silu(x)

def _sigmoid(x):
    return jax.nn.sigmoid(x)

def _layernorm(x, axis=-1, eps=1e-05):
    m = jnp.mean(x, axis=axis, keepdims=True)
    v = jnp.var(x, axis=axis, keepdims=True)
    return (x - m) / jnp.sqrt(v + eps)

def _scatter_add(tgt, idx, src, axis=0):
    return tgt.at[idx].add(src)

def _segment_sum(src, seg, n):
    return jax.ops.segment_sum(src, seg, n)
kernel_name = 'mk_gps_d1_gnn_r8_a6d809'

def setup_inputs(seed: int=0):
    np.random.seed(seed)
    _w = jnp.asarray

    def _rec_inputs():
        import jax
        import jax.numpy as jnp
        _gk = jax.random.key(seed)
        x = -0.0003713 + 1 * jax.random.normal(jax.random.fold_in(_gk, 1), (6250, 256), jnp.float32)
        src = jax.random.randint(jax.random.fold_in(_gk, 2), (200000,), 0, 6250, jnp.int32)
        dst = jax.random.randint(jax.random.fold_in(_gk, 3), (200000,), 0, 6250, jnp.int32)
        _o = jnp.argsort(dst, stable=True)
        src = src[_o]
        dst = dst[_o]
        return (x, src, dst)
    x, src, dst = _rec_inputs()

    def _L0_gnn_setup():
        import jax, jax.numpy as jnp
        import numpy as np
        N, IN_CH, HEADS, OUT_CH, E = (6250, 256, 4, 64, 100000)
        key = jax.random.key(seed)
        k1, k2, k3, k4, k5 = jax.random.split(key, 5)
        x = jax.random.normal(k1, (N, IN_CH), dtype=jnp.float32)
        edge_index = jax.random.randint(k2, (2, E), 0, N, dtype=jnp.int64)
        bw = float(np.sqrt(6.0 / (IN_CH + HEADS * OUT_CH)))
        ba = float(np.sqrt(6.0 / (HEADS + OUT_CH)))
        weight = jax.random.uniform(k3, (IN_CH, HEADS * OUT_CH), jnp.float32, -bw, bw)
        attn_l = jax.random.uniform(k4, (HEADS, OUT_CH), jnp.float32, -ba, ba)
        attn_r = jax.random.uniform(k5, (HEADS, OUT_CH), jnp.float32, -ba, ba)
        return {'x': x, 'edge_index': edge_index, 'weight': weight, 'attn_l': attn_l, 'attn_r': attn_r}
    _L0_gnn_all = _L0_gnn_setup()
    _L0_gnn_in = {k: v for k, v in _L0_gnn_all.items() if k in ('weight', 'attn_l', 'attn_r')}
    del _L0_gnn_all

    def _L0_mix_setup():
        import jax, jax.numpy as jnp
        import numpy as np
        A, Bc, Cc = (0.5, 1.0, 1.0)
        H = 8
        EPS = 1e-12

        def _normalize(t):
            n = jnp.linalg.norm(t, axis=-1, keepdims=True)
            return t / jnp.maximum(n, EPS)
        key = jax.random.key(seed)
        ks = jax.random.split(key, 5)
        B, N, C = (8, 256, 256)
        D = C // H
        x = jax.random.normal(ks[0], (B, N, C), dtype=jnp.float32)
        Wqkv = jax.random.normal(ks[1], (3 * H * D, C), dtype=jnp.float32) * 0.02
        bqkv = jnp.zeros((3 * H * D,), dtype=jnp.float32)
        Wproj = jax.random.normal(ks[2], (C, H * D), dtype=jnp.float32) * 0.02
        bproj = jnp.zeros((C,), dtype=jnp.float32)
        temperature = jnp.ones((1, H, 1, 1), dtype=jnp.float32)
        return {'x': x, 'Wqkv': Wqkv, 'bqkv': bqkv, 'Wproj': Wproj, 'bproj': bproj, 'temperature': temperature}
    _L0_mix_all = _L0_mix_setup()
    _L0_mix_in = {k: v for k, v in _L0_mix_all.items() if k in ('Wqkv', 'bqkv', 'Wproj', 'bproj', 'temperature')}
    del _L0_mix_all

    def _L0_ffn_setup():
        import math
        import jax, jax.numpy as jnp
        import numpy as np
        CAPACITY_FACTOR = 1.25
        key = jax.random.key(seed)
        ks = jax.random.split(key, 5)
        B, L, D, F, E = (8, 1024, 256, 1024, 8)
        h = jax.random.normal(ks[0], (B, L, D), dtype=jnp.float32)
        gate_w = jax.random.normal(ks[1], (D, E), dtype=jnp.float32) * 0.02
        gate_b = jnp.zeros((E,), dtype=jnp.float32)
        w1 = jax.random.normal(ks[2], (E, D, F), dtype=jnp.float32) * (1.0 / math.sqrt(D))
        b1 = jnp.zeros((E, F), dtype=jnp.float32)
        w2 = jax.random.normal(ks[3], (E, F, D), dtype=jnp.float32) * (1.0 / math.sqrt(F))
        b2 = jnp.zeros((E, D), dtype=jnp.float32)
        return {'h': h, 'gate_w': gate_w, 'gate_b': gate_b, 'w1': w1, 'b1': b1, 'w2': w2, 'b2': b2}
    _L0_ffn_all = _L0_ffn_setup()
    _L0_ffn_in = {k: v for k, v in _L0_ffn_all.items() if k in ('gate_w', 'gate_b', 'w1', 'b1', 'w2', 'b2')}
    del _L0_ffn_all
    return {'x': x, 'src': src, 'dst': dst, 'L0_gnn_weight': _L0_gnn_in['weight'], 'L0_gnn_attn_l': _L0_gnn_in['attn_l'], 'L0_gnn_attn_r': _L0_gnn_in['attn_r'], 'L0_mix_Wqkv': _L0_mix_in['Wqkv'], 'L0_mix_bqkv': _L0_mix_in['bqkv'], 'L0_mix_Wproj': _L0_mix_in['Wproj'], 'L0_mix_bproj': _L0_mix_in['bproj'], 'L0_mix_temperature': _L0_mix_in['temperature'], 'L0_ffn_gate_w': _L0_ffn_in['gate_w'], 'L0_ffn_gate_b': _L0_ffn_in['gate_b'], 'L0_ffn_w1': _L0_ffn_in['w1'], 'L0_ffn_b1': _L0_ffn_in['b1'], 'L0_ffn_w2': _L0_ffn_in['w2'], 'L0_ffn_b2': _L0_ffn_in['b2']}

def reference(x, src, dst, L0_gnn_weight, L0_gnn_attn_l, L0_gnn_attn_r, L0_mix_Wqkv, L0_mix_bqkv, L0_mix_Wproj, L0_mix_bproj, L0_mix_temperature, L0_ffn_gate_w, L0_ffn_gate_b, L0_ffn_w1, L0_ffn_b1, L0_ffn_w2, L0_ffn_b2):
    import jax
    import jax.numpy as jnp

    def _L0_gnn_ref(x, edge_index, weight, attn_l, attn_r):
        import jax, jax.numpy as jnp
        import numpy as np
        N, IN_CH, HEADS, OUT_CH, E = (6250, 256, 4, 64, 100000)
        heads, out_ch = attn_l.shape
        n = x.shape[0]
        xt = jnp.matmul(x, weight).reshape(-1, heads, out_ch)
        row, col = (edge_index[0], edge_index[1])
        alpha_l = jnp.einsum('ehd,hd->eh', xt[row], attn_l)
        alpha_r = jnp.einsum('ehd,hd->eh', xt[col], attn_r)
        alpha = jax.nn.softmax(jax.nn.leaky_relu(alpha_l + alpha_r, 0.01), axis=1)
        tmp = jnp.einsum('nh,nhd->nd', alpha[:n], xt[col[:n]])
        out = jnp.broadcast_to(tmp[:, None, :], (n, heads, out_ch))
        return out.reshape(n, heads * out_ch)

    def _L0_mix_ref(x, Wqkv, bqkv, Wproj, bproj, temperature):
        import jax, jax.numpy as jnp
        import numpy as np
        A, Bc, Cc = (0.5, 1.0, 1.0)
        H = 8
        EPS = 1e-12

        def _normalize(t):
            n = jnp.linalg.norm(t, axis=-1, keepdims=True)
            return t / jnp.maximum(n, EPS)
        B, N, C = x.shape
        D = C // H
        scale = float(D) ** 0.25
        qkv = (x @ Wqkv.T + bqkv).reshape(B, N, 3, H, D)
        qkv = jnp.transpose(qkv, (2, 0, 3, 1, 4))
        q, k, v = (qkv[0], qkv[1], qkv[2])
        q = q * scale
        v1 = jnp.concatenate([jnp.ones((B, H, N, 1), dtype=v.dtype), v], axis=-1)
        qn = _normalize(q) * (scale * temperature)
        kn = _normalize(k) * scale
        vN = v1 / N
        kv_mod = jnp.einsum('bhni,bhnj,bhne->bhije', kn, kn, vN)
        kv = jnp.einsum('bhnd,bhne->bhde', kn, vN)
        vsum = jnp.sum(vN, axis=-2)[:, :, None, :]
        y = A * jnp.einsum('bhni,bhnj,bhije->bhne', qn, qn, kv_mod) + scale ** 2 * Bc * jnp.einsum('bhnd,bhde->bhne', qn, kv) + scale ** 4 * Cc * vsum
        y_norm, y = (y[..., :1], y[..., 1:])
        y = y / y_norm
        out = jnp.transpose(y, (0, 2, 1, 3)).reshape(B, N, H * D)
        return out @ Wproj.T + bproj

    def _L0_ffn_ref(h, gate_w, gate_b, w1, b1, w2, b2):
        import math
        import jax, jax.numpy as jnp
        import numpy as np
        CAPACITY_FACTOR = 1.25
        B, L, D = h.shape
        E = gate_w.shape[1]
        T = B * L
        C = max(1, math.ceil(CAPACITY_FACTOR * T / E))
        x = h.reshape(T, D)
        logits = x @ gate_w + gate_b
        probs = jax.nn.softmax(logits, axis=-1)
        idx = jnp.argmax(probs, axis=-1)
        prb = jnp.take_along_axis(probs, idx[:, None], axis=1)[:, 0]
        one_hot = jax.nn.one_hot(idx, E, dtype=jnp.float32)
        pos = (jnp.cumsum(one_hot, axis=0) * one_hot).sum(-1).astype(jnp.int32) - 1
        kept = pos < C
        pos_safe = jnp.where(kept, pos, C)
        buf = jnp.zeros((E, C, D), dtype=h.dtype).at[idx, pos_safe].set(x, mode='drop')
        hmid = jax.nn.relu(jnp.einsum('ecd,edf->ecf', buf, w1) + b1[:, None, :])
        ybuf = jnp.einsum('ecf,efd->ecd', hmid, w2) + b2[:, None, :]
        pos_g = jnp.minimum(pos, C - 1)
        y_tok = ybuf[idx, pos_g] * (prb * kept)[:, None]
        y = y_tok.reshape(B, L, D)
        y = jnp.nan_to_num(y, nan=0.0, posinf=10000.0, neginf=-10000.0)
        return y
    edge_index = jnp.stack([src, dst])
    xn = _layernorm(x, axis=-1)
    x = x + _L0_gnn_ref(xn, edge_index, L0_gnn_weight, L0_gnn_attn_l, L0_gnn_attn_r) + _L0_mix_ref(xn[None], L0_mix_Wqkv, L0_mix_bqkv, L0_mix_Wproj, L0_mix_bproj, L0_mix_temperature)[0]
    x = x + _L0_ffn_ref(_layernorm(x, axis=-1)[None], L0_ffn_gate_w, L0_ffn_gate_b, L0_ffn_w1, L0_ffn_b1, L0_ffn_w2, L0_ffn_b2)[0]
    return x

_drawn_inputs = setup_inputs


def setup_inputs(seed=0):
    import zlib

    import numpy as np

    out = dict(_drawn_inputs(seed))
    spreads = {'L0_mix_bqkv': (0.0, 0.1),
     'L0_mix_bproj': (0.0, 0.1),
     'L0_mix_temperature': (1.0, 0.6),
     'L0_ffn_gate_b': (0.0, 0.1),
     'L0_ffn_b1': (0.0, 0.713),
     'L0_ffn_b2': (0.0, 0.505)}
    factors = {'L0_mix_Wqkv': 21.763}
    for name, (base, spread) in spreads.items():
        noise = np.random.default_rng([zlib.crc32(name.encode()), seed]).standard_normal(out[name].shape)
        drawn = base * np.exp(spread * noise) if base else spread * noise
        out[name] = jnp.asarray(drawn.astype(out[name].dtype))
    for name, factor in factors.items():
        out[name] = (out[name] * factor).astype(out[name].dtype)
    return out
```

```python
from contextlib import ExitStack

import numpy as np

import concourse.bass as bass
from concourse import mybir

F32 = mybir.dt.float32
F32R = mybir.dt.float32r
I32 = mybir.dt.int32
U32 = mybir.dt.uint32
ALU = mybir.AluOpType
ACT = mybir.ActivationFunctionType
AX_X = mybir.AxisListType.X

N, D = 6250, 256
PT, TILES = 125, 50
PAIRS, NP = TILES // 2, 2 * PT
GH, GD = 4, 64
H, HD = 8, 32
G, R = 2, 4
ND = HD // 2
NF = ND * HD
CH = NF // 128
E, F = 8, 1024
CAP = -(-5 * N // (4 * E))
SP_, SI = 123, 8
SLOTS = SP_ * SI
HALF = SI // 2 * SP_
FC = F // 128
LN_EPS = 1e-5
EPS = 1e-12
SCALE = float(HD) ** 0.25
WC = 3 * D + D + 2 * GH
KVW = 1 + HD + HD + ND
GW = NF + ND + 1
TW = D + GH
MEAN, VAR, RSTD, GATE, TOKEN, RW = D, D + 1, D + 2, D + 3, D + 4, D + 5
NO_TOKEN = 65536.0
LIN = 1 + 2 * HD

C_ID, C_BLK, C_TRI, C_M4, C_M8 = 0, 128, 256, 384, 388
C_REV, C_TOK = 404, 420
C_SEL, C_SEL5, NC_ = 470, 470 + 8 * 128, 470 + 12 * 128


def constants():
    c = np.zeros((128, NC_), np.float32)
    p = np.arange(128)
    c[:, C_ID:C_ID + 128] = np.eye(128)
    c[:, C_BLK:C_BLK + 128] = (p[:, None] // HD) == (p[None] // HD)
    c[:, C_TRI:C_TRI + 128] = p[:, None] <= p[None]
    c[:, C_M4:C_M4 + R] = (p[:, None] // HD) == np.arange(R)
    for g in range(G):
        c[:, C_M8 + 8 * g:C_M8 + 8 * g + 8] = (p[:, None] // HD + R * g) == np.arange(H)
    c[:, C_REV:C_REV + E] = E - np.arange(E)
    c[0:PT, C_TOK:C_TOK + TILES] = np.arange(N).reshape(TILES, PT).T
    for hp in range(2):
        for ch in range(CH):
            for f in range(128):
                d, i = divmod(ch * 128 + f, HD)
                for part in range(2):
                    for x in {i, (i + d) % HD}:
                        c[hp * 64 + part * HD + x, C_SEL + (hp * CH + ch) * 128 + f] = 1
    for b in range(H // 2):
        for hp in range(2):
            for i in range(ND):
                for part in range(2):
                    for x in (i, i + ND):
                        c[hp * 64 + part * HD + x, C_SEL5 + b * 128 + (2 * b + hp) * ND + i] = 1
    return c


def wait(eng, sem, n):
    if not (isinstance(n, int) and n <= 0):
        eng.wait_ge(sem, n)


def inside(t, count):
    return not isinstance(t, int) or 0 <= t < count


def pipeline(eng, first, last, loop_from, loop_to, step, turn=2):
    def div(t):
        return lambda d, n: (t + d) // n

    for t in range(first, loop_from):
        step(t, t % turn, div(t))
    with eng.Fori(0, (loop_to - loop_from) // turn) as i:
        for u in range(turn):
            t = loop_from + u
            step(i * turn + t, t % turn, lambda d, n, t=t: i * (turn // n) + (t + d) // n)
    for t in range(loop_to, last):
        step(t, t % turn, div(t))


def view(ap, offset, dims):
    return bass.AP(tensor=ap.tensor, offset=ap.offset + offset, ap=[list(ap.ap[0])] + dims)


def build(nc, x, src, dst, wg, attn_l, attn_r, wqkvT, bqkv, wprojT, bproj, temp, gate_w, gate_b, w1, b1, w2, b2,
          consts, out, table, alr_table, slots):
    x_v = x.rearrange("(t p) d -> p t d", p=PT)
    out_v = out.rearrange("(t p) d -> p t d", p=PT)
    table_v = table.rearrange("(t p) d -> p t d", p=PT)
    alr_v = alr_table.rearrange("(t p) d -> p t d", p=PT)

    with ExitStack() as whole:
        def sem(name):
            return whole.enter_context(nc.semaphore(name))

        cst = whole.enter_context(nc.sbuf_tensor("cst", [128, C_SEL], F32))
        ident = cst[:, C_ID:C_ID + 128]
        with ExitStack() as nodes:
            def keep(name, shape, dt=F32):
                return nodes.enter_context(nc.sbuf_tensor(name, shape, dt))

            x_all = keep("x_all", [PT, TILES, D])
            q_all = keep("q_all", [PT, TILES, D])
            idx_all = keep("idx_all", [PT, 2, TILES], I32)
            coef = keep("coef", [128, G, CH, 128])
            coef5 = keep("coef5", [128, G, 128])
            lin = keep("lin", [128, G, 128])
            gram = keep("gram", [128, G, 128])
            sums = keep("sums", [128, 2 * 66 + 2 * 18])
            build_a(nc, sem, ExitStack(), x_v, src, dst, wg, attn_l, attn_r, wqkvT, bqkv, temp, consts, table_v, alr_v,
                    slots, x_all, q_all, idx_all, cst, ident, coef, coef5, lin, gram, sums)
            build_b(nc, sem, ExitStack(), wprojT, bproj, gate_w, gate_b, consts, table, alr_table, out_v, slots,
                    x_all, q_all, idx_all, cst, ident, coef, coef5, lin, gram, sums)
        build_experts(nc, sem, ExitStack(), w1, b1, w2, b2, slots, out, ident)


def build_a(nc, sem, scope, x_v, src, dst, wg, attn_l, attn_r, wqkvT, bqkv, temp, consts, table_v, alr_v, slots,
            x_all, q_all, idx_all, cst, ident, coef, coef5, lin, gram, sums):
    with scope:
        def sb(name, shape, dt=F32):
            return scope.enter_context(nc.sbuf_tensor(name, shape, dt))

        def ps(name):
            return scope.enter_context(nc.psum_tensor(name, [128, 512], F32))

        w_raw = sb("w_raw", [128, 2, WC])
        w_hi = sb("w_hi", [128, 2, WC], F32R)
        w_lo = sb("w_lo", [128, 2, WC], F32R)
        b_raw = q_all[0:2, 40:43, :].rearrange("p t d -> p (t d)")
        b_hi = sb("b_hi", [2, 3 * D], F32R)
        b_lo = q_all[0:2, 43:46, :].rearrange("p t d -> p (t d)")
        b_two = sb("b_two", [2, 3 * D], F32R)
        ones2 = sb("ones2", [2, PT], F32R)
        floor2 = sb("floor2", [PT, 2 * H])
        gain = sb("gain", [PT, 2 * H])
        eps_t = sb("eps_t", [PT, 1])
        FILLS_A, BI_A = 24, 4
        BLANK = E * SLOTS // FILLS_A
        blank = sb("blank", [BLANK // BI_A, BI_A, RW])
        idx_raw = q_all[0:TILES, 46, 0:2 * PT].rearrange("t (n p) -> t n p", n=2).bitcast(I32)
        idx_f = q_all[0:TILES, 47, 0:2 * PT].rearrange("t (n p) -> t n p", n=2)
        stats = sb("stats", [PT, 2, 6])
        mv = sb("mv", [PT, 4, 2])
        std = sb("std", [PT, 2])
        rstd = sb("rstd", [PT, 2])
        xn = sb("xn", [PT, 2, D])
        xT_hi = sb("xT_hi", [128, 2, 2, PT], F32R)
        xT_lo = sb("xT_lo", [128, 2, 2, PT], F32R)
        qk_full = sb("qk", [128, 2, 2 * D])
        sq_full = sb("qk_sq", [128, 2, 2 * D])
        qk, qk_sq = qk_full[0:PT], sq_full[0:PT]
        attn, attn_w = qk_full[:, 0, :].rearrange("p (a n) -> p a n", a=2), sq_full[:, 0, :].rearrange("p (a n) -> p a n", a=2)
        ss = sb("ss", [PT, 2, 2 * H])
        ssm = sb("ssm", [PT, 2, 2 * H])
        norm = sb("norm", [PT, 2, 2 * H])
        rnorm = sb("rnorm", [PT, 2, 2 * H])
        fac = sb("fac", [PT, 2, 2 * H])
        kv = sb("kv", [PT, 2, H, KVW])
        feat_full = sb("feat", [128, 2, H, GW])
        feat = feat_full[0:PT]
        rest = feat_full[:].rearrange("p s h w -> p (s h w)")
        t_st = sb("t_st", [PT, 2, TW])
        alr = sb("alr", [PT, TILES, 2 * GH])
        acc_sb = rest[:, 0:G * NF].rearrange("p (g f) -> p g f", g=G)
        pad = rest[:, G * NF:G * NF + G * (ND - 1) * 2 * HD].rearrange("p (g d i) -> p g d i", g=G, d=ND - 1)
        dsum = sb("dsum", [128, G, 3, HD])
        x5 = sb("x5", [128, G, H, ND])

        p_t = [ps("p_t0"), ps("p_t1")]
        p_qk = [ps("p_qk0"), ps("p_qk1")]
        p_vx = ps("p_vx")
        p_acc = [ps("p_acc0"), ps("p_acc1")]
        p_sum = ps("p_sum")

        s_cst, s_w, s_attn, s_bias, s_temp = sem("s_cst"), sem("s_w"), sem("s_attn"), sem("s_bias"), sem("s_temp")
        s_init, s_zero = sem("s_init"), sem("s_zero")
        s_ild, s_if, s_it, s_idx_a = sem("s_ild"), sem("s_if"), sem("s_it"), sem("s_idx_a")
        s_prep, s_whi = sem("s_prep"), sem("s_whi")
        s_x = [sem("s_x0"), sem("s_x1")]
        s_stat, s_mv, s_std, s_rstd, s_xn = sem("s_stat"), sem("s_mv"), sem("s_std"), sem("s_rstd"), sem("s_xn")
        s_tp, s_hi, s_lo = sem("s_tp"), sem("s_hi"), sem("s_lo")
        s_alrmm, s_qkmm, s_vxmm = sem("s_alrmm"), sem("s_qkmm"), sem("s_vxmm")
        s_alr, s_ar, s_qk, s_v, s_xt = sem("s_alr"), sem("s_ar"), sem("s_qk"), sem("s_v"), sem("s_xt")
        s_sq, s_ss, s_ssm, s_norm, s_rn, s_fac = (sem("s_sq"), sem("s_ss"), sem("s_ssm"), sem("s_norm"),
                                                  sem("s_rn"), sem("s_fac"))
        s_kn, s_qn, s_wrap, s_d16, s_kk, s_kv = (sem("s_kn"), sem("s_qn"), sem("s_wrap"), sem("s_d16"),
                                                 sem("s_kk"), sem("s_kv"))
        s_tst = [sem("s_tst0"), sem("s_tst1")]
        s_alrst = sem("s_alrst")
        s_kkp = sem("s_kkp")
        s_met = [sem("s_met_dve"), sem("s_met_pool")]
        s_fin, s_ct = sem("s_fin"), sem("s_ct")
        W_READY = 10

        PH = 2

        def pairs(eng, u, g, r0, r1):
            k = kv[:, u, R * g + r0:R * g + r0 + 1, 1 + HD:2 + HD]
            return eng.tensor_tensor(
                feat[:, u, R * g + r0:R * g + r1, 0:NF].rearrange("p h (d i) -> p h d i", d=ND),
                view(k, 0, [[KVW, r1 - r0], [0, ND], [1, HD]]), view(k, 0, [[KVW, r1 - r0], [1, ND], [1, HD]]), ALU.mult)

        def run(eng, first, last, step):
            pipeline(eng, first, last, 4, 46, step)

        with nc.Block() as block:
            @block.sync
            def _(sp):
                sp.dma_start(x_all[:, 0, :], x_v[:, 0, :]).then_inc(s_x[0], 16)
                sp.dma_start(w_raw[:, :, 3 * D:4 * D], wg.rearrange("(k p) n -> p k n", p=128)).then_inc(s_w, 16)
                sp.dma_start(w_raw[:, :, 0:3 * D], wqkvT.rearrange("(k p) n -> p k n", p=128)).then_inc(s_w, 16)
                sp.dma_start(x_all[:, 1, :], x_v[:, 1, :]).then_inc(s_x[1], 16)
                sp.dma_start(b_raw, bqkv.partition_broadcast(2)).then_inc(s_bias, 16)
                sp.wait_ge(s_init, 3)
                sp.dma_start(gain[:, 0:H], temp.partition_broadcast(PT)).then_inc(s_temp, 16)

                for t in (2, 3):
                    sp.wait_ge(s_x[t % 2], 16)
                    sp.dma_start(x_all[:, t, :], x_v[:, t, :]).then_inc(s_x[t % 2], 16)

                def step(t, u, div):
                    if u == 0 and inside(t, 2 * FILLS_A):
                        sp.dma_start(slots[bass.ds(t * (BLANK // 2), BLANK), :].rearrange("(p i) d -> p i d", i=BI_A),
                                     blank[:]).then_inc(s_zero, 16)
                    if inside(t + 4, TILES):
                        sp.wait_ge(s_x[u], (div(0, 2) + 2) * 16)
                        sp.dma_start(x_all[:, t + 4, :], x_v[:, t + 4, :]).then_inc(s_x[u], 16)
                    if inside(t - 1, TILES):
                        sp.wait_ge(s_xt, t)
                        sp.wait_ge(s_ar, t)
                        sp.dma_start(table_v[:, t - 1, :], t_st[:, 1 - u, :]).then_inc(s_tst[1 - u], 16)
                run(sp, 0, TILES + 1, step)
                sp.wait_ge(s_alr, TILES)
                sp.dma_start(alr_v, alr[:]).then_inc(s_alrst, 16)
                sp.wait_ge(s_alrst, 16)
                sp.wait_ge(s_zero, 16 * FILLS_A)
                sp.wait_ge(s_tst[0], 16 * TILES // 2)
                sp.wait_ge(s_tst[1], 16 * TILES // 2)

            @block.gpsimd
            def _(pool):
                pool.memset(blank[:, :, 0:TOKEN], 0.0).then_inc(s_init, 1)
                pool.memset(blank[:, :, TOKEN:RW], NO_TOKEN).then_inc(s_init, 1)
                pool.memset(gain[:], 1.0).then_inc(s_init, 1)
                pool.memset(eps_t[:], LN_EPS).then_inc(s_init, 1)
                pool.memset(floor2[:, 0:H], (EPS / SCALE) ** 2).then_inc(s_init, 1)
                pool.memset(floor2[:, H:2 * H], EPS ** 2).then_inc(s_init, 1)
                pool.memset(kv[:, :, :, 0:1], 1.0).then_inc(s_init, 1)
                pool.memset(feat[:, :, :, GW - 1:GW], 1.0).then_inc(s_init, 1)

                def step(t, u, div):
                    pool.wait_ge(s_fac, t + 1)
                    pool.wait_ge(s_qk, t + 1)
                    wait(pool, s_kv, t - 1)
                    wait(pool, s_kk, 2 * (t - 1))
                    k = kv[:, u, :, 1 + HD:1 + 2 * HD]
                    pool.tensor_tensor(k, qk[:, u, D:2 * D].rearrange("p (h d) -> p h d", h=H),
                                       fac[:, u, H:2 * H].unsqueeze(2).to_broadcast([PT, H, HD]),
                                       ALU.mult).then_inc(s_kn, 1)
                    pool.wait_ge(s_kn, t + 1)
                    pool.sem_inc(s_met[1], 1)
                    pool.tensor_scalar(kv[:, u, :, 1 + 2 * HD:KVW], kv[:, u, :, 1 + HD:1 + HD + ND], 1.0, None,
                                       ALU.mult).then_inc(s_wrap, 1)
                    pool.wait_ge(s_wrap, t + 1)
                    pairs(pool, u, 1, PH, R).then_inc(s_kkp, 1)
                    pool.tensor_tensor(feat[:, u, :, NF:NF + ND], kv[:, u, :, 1 + HD:1 + HD + ND],
                                       kv[:, u, :, 1 + HD + ND:1 + 2 * HD], ALU.mult).then_inc(s_d16, 1)
                    pool.tensor_tensor(q_all[:, t, :].rearrange("p (h d) -> p h d", h=H),
                                       qk[:, u, 0:D].rearrange("p (h d) -> p h d", h=H),
                                       fac[:, u, 0:H].unsqueeze(2).to_broadcast([PT, H, HD]),
                                       ALU.mult).then_inc(s_qn, 1)
                run(pool, 0, TILES, step)
                pool.wait_ge(s_qn, TILES)

            @block.scalar
            def _(act):
                for n, a in enumerate((attn_r, attn_l)):
                    act.dma_start(attn[:, n, :], a.partition_broadcast(128)).then_inc(s_attn, 16)
                for n, a in enumerate((src, dst)):
                    act.dma_start(idx_raw[:, n, :], a.rearrange("(t p) -> t p", p=PT)).then_inc(s_ild, 16)
                act.dma_start(cst[:], consts[:, 0:C_SEL]).then_inc(s_cst, 16)
                act.wait_ge(s_w, 32)
                act.wait_ge(s_prep, 4)
                act.activation(w_hi[:], w_raw[:], ACT.Copy).then_inc(s_whi, 1)
                act.wait_ge(s_init, 8)

                def step(t, u, div):
                    if inside(t, TILES):
                        act.wait_ge(s_alrmm, t + 1)
                        act.activation(alr[:, t, :], p_t[u][0:PT, 2 * PT:2 * PT + 2 * GH], ACT.Copy).then_inc(s_alr, 1)
                        wait(act, s_tst[u], div(0, 2) * 16)
                        act.activation(t_st[:, u, D:TW], p_t[u][0:PT, 2 * PT:2 * PT + GH], ACT.Copy).then_inc(s_ar, 1)
                    if inside(t + 1, TILES):
                        act.wait_ge(s_tp, t + 2)
                        wait(act, s_vxmm, t)
                        wait(act, s_lo, t)
                        act.activation(xT_hi[:, 1 - u, :, :].rearrange("p k n -> p (k n)"),
                                       p_t[1 - u][:, 0:2 * PT], ACT.Copy).then_inc(s_hi, 1)
                    if inside(t, TILES):
                        act.wait_ge(s_qkmm, t + 1)
                        wait(act, s_qn, t - 1)
                        act.activation(qk[:, u, :], p_qk[u][0:PT, :], ACT.Copy).then_inc(s_qk, 1)
                        act.wait_ge(s_qk, t + 1)
                        wait(act, s_ss, t - 1)
                        act.activation(qk_sq[:, u, :], qk[:, u, :], ACT.Square).then_inc(s_sq, 1)
                        act.wait_ge(s_ssm, t + 1)
                        wait(act, s_rn, t - 1)
                        act.activation(norm[:, u, :], ssm[:, u, :], ACT.Sqrt).then_inc(s_norm, 1)
                        act.wait_ge(s_vxmm, t + 1)
                        wait(act, s_kv, t - 1)
                        act.activation(kv[:, u, :, 1:1 + HD],
                                       p_vx[0:PT, 0:D].rearrange("p (h d) -> p h d", h=H), ACT.Copy).then_inc(s_v, 1)
                        act.activation(t_st[:, u, 0:D], p_vx[0:PT, D:2 * D], ACT.Copy).then_inc(s_xt, 1)
                    if inside(t + 3, TILES):
                        act.wait_ge(s_mv, t + 4)
                        wait(act, s_rstd, t + 2)
                        act.activation(std[:, 1 - u:2 - u], mv[:, 1 - u, 1:2], ACT.Sqrt,
                                       bias=eps_t[:, 0:1]).then_inc(s_std, 1)
                run(act, -3, TILES, step)

            @block.tensor
            def _(pe):
                pe.wait_ge(s_cst, 16)
                pe.wait_ge(s_init, 8)
                pe.wait_ge(s_if, 1)
                for n in range(2):
                    mm = pe.transpose(p_acc[0][0:PT, n * TILES:(n + 1) * TILES], idx_f[:, n, :], ident[0:TILES, 0:TILES])
                mm.then_inc(s_it, 1)
                pe.wait_ge(s_idx_a, 1)
                pe.wait_ge(s_whi, 1)
                pe.wait_ge(s_prep, W_READY)

                def project(bank, t, u, c0, c1, done, bias):
                    n = c1 - c0
                    passes = [(xT, w, k) for k in range(2) for xT, w in ((xT_hi, w_hi), (xT_hi, w_lo), (xT_lo, w_hi))]
                    for i, (xT, w, k) in enumerate(passes):
                        last = i == len(passes) - 1
                        mm = pe.matmul(bank[0:PT, 0:n] if n > 2 * GH else bank[0:PT, 2 * PT:2 * PT + n],
                                       xT[:, u, k, :], w[:, k, c0:c1], start=i == 0, stop=last)
                        if bias and i == 0:
                            pe.matmul(bank[0:PT, 0:bias], ones2[:], b_two[:, c0:c0 + bias], start=False, stop=False)
                    mm.then_inc(done, 1)

                def step(t, u, div):
                    if inside(t, TILES):
                        pe.wait_ge(s_hi, t + 1)
                        pe.wait_ge(s_lo, t + 1)
                        project(p_t[u], t, u, 4 * D, WC, s_alrmm, 0)
                    if inside(t + 1, TILES):
                        pe.wait_ge(s_xn, t + 2)
                        wait(pe, s_alr, t)
                        wait(pe, s_ar, t)
                        for k in range(2):
                            mm = pe.transpose(p_t[1 - u][:, k * PT:(k + 1) * PT], xn[:, 1 - u, k * 128:(k + 1) * 128],
                                              ident[0:PT, 0:PT])
                        mm.then_inc(s_tp, 1)
                    if inside(t, TILES):
                        wait(pe, s_qk, t - 1)
                        project(p_qk[u], t, u, 0, 2 * D, s_qkmm, 2 * D)
                    if inside(t - 2, TILES):
                        pe.wait_ge(s_kk, 2 * (t - 1))
                        pe.wait_ge(s_kkp, t - 1)
                        pe.wait_ge(s_d16, t - 1)
                        pe.wait_ge(s_v, t - 1)
                        first = isinstance(t, int) and t == 2
                        last = isinstance(t, int) and t == TILES + 1
                        for g in range(G):
                            for r in range(R):
                                q = slice(HD * r, HD * r + HD)
                                pe.matmul(p_acc[g][q, :], kv[:, u, R * g + r, 1:1 + HD], feat[:, u, R * g + r, 0:NF],
                                          start=first, stop=last, skip_group_check=True)
                            for r in range(R):
                                q = slice(HD * r, HD * r + HD)
                                pe.matmul(p_sum[q, 66 * g:66 * g + LIN], kv[:, u, R * g + r, 1 + HD:1 + 2 * HD],
                                          kv[:, u, R * g + r, 0:LIN], start=first and g == 0, stop=last,
                                          skip_group_check=True)
                            for r in range(R):
                                q = slice(HD * r, HD * r + HD)
                                mm = pe.matmul(p_sum[q, 132 + 18 * g:132 + 18 * g + ND + 1],
                                               kv[:, u, R * g + r, 1:1 + HD], feat[:, u, R * g + r, NF:GW],
                                               start=False, stop=last, skip_group_check=True)
                        mm.then_inc(s_kv, 1)
                    if inside(t, TILES):
                        wait(pe, s_v, t)
                        wait(pe, s_xt, t)
                        project(p_vx, t, u, 2 * D, 4 * D, s_vxmm, D)
                run(pe, -1, TILES + 2, step)
                pe.wait_ge(s_xt, TILES)
                for g in range(G):
                    for c in range(CH):
                        if c == 0:
                            pe.wait_ge(s_fin, FIN_ACC[g])
                        mm = pe.transpose(p_t[g][:, c * 128:(c + 1) * 128], acc_sb[:, g, c * 128:(c + 1) * 128], ident)
                    mm.then_inc(s_ct, 1)
                pe.wait_ge(s_fin, FIN_X5)
                for g in range(G):
                    mm = pe.transpose(p_vx[:, g * 128:(g + 1) * 128], x5[:, g, :, :].rearrange("p h i -> p (h i)"),
                                      ident)
                mm.then_inc(s_ct, 1)

            @block.vector
            def _(dve):
                n = [0]

                def link(ins, done):
                    n[0] += 1
                    ins.then_inc(done, 1)
                    dve.wait_ge(done, n[0])

                dve.wait_ge(s_ild, 32)
                dve.tensor_copy(idx_f, idx_raw).then_inc(s_if, 1)
                dve.wait_ge(s_it, 1)
                dve.tensor_copy(idx_all[:].rearrange("p n t -> p (n t)"), p_acc[0][0:PT, 0:2 * TILES]).then_inc(s_idx_a, 1)
                dve.wait_ge(s_w, 32)
                dve.wait_ge(s_attn, 32)
                for a in range(2):
                    aw = attn[:, a, :].unsqueeze(1).to_broadcast([128, 2, D])
                    link(dve.tensor_tensor(attn_w, w_raw[:, :, 3 * D:4 * D], aw, ALU.mult), s_prep)
                    link(dve.tensor_reduce(w_raw[:, :, 4 * D + GH * a:4 * D + GH * a + GH],
                                           attn_w.rearrange("p k (h d) -> p k h d", h=GH), AX_X, ALU.add), s_prep)
                dve.wait_ge(s_bias, 16)
                dve.wait_ge(s_cst, 16)
                link(dve.tensor_copy(b_hi[:], b_raw), s_prep)
                link(dve.tensor_tensor(b_lo, b_raw, b_hi[:].bitcast(F32), ALU.subtract), s_prep)
                link(dve.tensor_scalar(b_raw, b_hi[:].bitcast(F32), ident[0:2, 0:1], None, ALU.mult), s_prep)
                dve.scalar_tensor_tensor(out=b_two[:], in0=b_lo, scalar=ident[0:2, 1:2], in1=b_raw,
                                         op0=ALU.mult, op1=ALU.add).then_inc(s_prep, 1)
                dve.tensor_copy(ones2[:], cst[0:2, C_BLK:C_BLK + 1].to_broadcast([2, PT])).then_inc(s_prep, 1)
                dve.wait_ge(s_whi, 1)
                dve.tensor_tensor(w_lo[:], w_raw[:], w_hi[:].bitcast(F32), ALU.subtract).then_inc(s_prep, 1)
                dve.wait_ge(s_temp, 16)
                dve.wait_ge(s_init, 8)

                def step(t, u, div):
                    if inside(t + 2, TILES):
                        dve.wait_ge(s_std, t + 3)
                        wait(dve, s_xn, t + 1)
                        dve.reciprocal(rstd[:, u:u + 1], std[:, u:u + 1]).then_inc(s_rstd, 1)
                    if inside(t + 1, TILES):
                        dve.wait_ge(s_hi, t + 2)
                        wait(dve, s_vxmm, t)
                        dve.tensor_tensor(xT_lo[:, 1 - u, :, :].rearrange("p k n -> p (k n)"), p_t[1 - u][:, 0:2 * PT],
                                          xT_hi[:, 1 - u, :, :].rearrange("p k n -> p (k n)").bitcast(F32),
                                          ALU.subtract).then_inc(s_lo, 1)
                    if inside(t - 1, TILES):
                        dve.wait_ge(s_wrap, t)
                        wait(dve, s_kv, t - 2)
                        pairs(dve, 1 - u, 0, 0, R).then_inc(s_kk, 1)
                    if inside(t, TILES):
                        dve.wait_ge(s_sq, t + 1)
                        dve.tensor_reduce(ss[:, u, :], qk_sq[:, u, :].rearrange("p (h d) -> p h d", d=HD), AX_X,
                                          ALU.add).then_inc(s_ss, 1)
                    if inside(t + 3, TILES):
                        dve.wait_ge(s_x[1 - u], 16 * (div(0, 2) + 2 + u))
                        dve.bn_stats(stats[:, 1 - u, :], x_all[:, t + 3, :]).then_inc(s_stat, 1)
                    if inside(t, TILES):
                        dve.wait_ge(s_ss, t + 1)
                        wait(dve, s_norm, t - 1)
                        dve.tensor_tensor(ssm[:, u, :], ss[:, u, :], floor2[:], ALU.max).then_inc(s_ssm, 1)
                    if inside(t + 2, TILES):
                        dve.wait_ge(s_rstd, t + 3)
                        wait(dve, s_tp, t + 1)
                        dve.tensor_scalar(xn[:, u, :], x_all[:, t + 2, :], mv[:, u, 0:1], rstd[:, u:u + 1],
                                          ALU.subtract, ALU.mult).then_inc(s_xn, 1)
                    if inside(t + 3, TILES):
                        dve.wait_ge(s_stat, t + 4)
                        wait(dve, s_std, t + 2)
                        wait(dve, s_xn, t + 2)
                        dve.sem_inc(s_met[0], 1)
                        dve.bn_aggr(mv[:, 1 - u, :], stats[:, 1 - u, :]).then_inc(s_mv, 1)
                    if inside(t, TILES):
                        dve.wait_ge(s_norm, t + 1)
                        wait(dve, s_fac, t - 1)
                        dve.reciprocal(rnorm[:, u, :], norm[:, u, :]).then_inc(s_rn, 1)
                    if inside(t, TILES):
                        dve.wait_ge(s_rn, t + 1)
                        wait(dve, s_qn, t - 1)
                        wait(dve, s_kn, t - 1)
                        dve.tensor_tensor(fac[:, u, :], rnorm[:, u, :], gain[:], ALU.mult).then_inc(s_fac, 1)
                    if inside(t - 1, TILES):
                        pairs(dve, 1 - u, 1, 0, PH).then_inc(s_kk, 1)
                run(dve, -3, TILES + 1, step)

                n[0] = 0
                dve.wait_ge(s_kv, TILES)
                for g in range(G):
                    link(dve.tensor_copy(sums[:, 66 * g:66 * g + LIN], p_sum[:, 66 * g:66 * g + LIN]), s_fin)
                    s16 = slice(132 + 18 * g, 132 + 18 * g + ND + 1)
                    link(dve.tensor_copy(sums[:, s16], p_sum[:, s16]), s_fin)
                for g in range(G):
                    link(dve.tensor_copy(acc_sb[:, g, :], p_acc[g][:, :]), s_fin)
                    acc = acc_sb[:, g, HD:NF].rearrange("p (d i) -> p d i", i=HD)
                    link(dve.tensor_copy(pad[:, g, :, 0:HD], acc), s_fin)
                    link(dve.tensor_copy(pad[:, g, :, HD:2 * HD], acc), s_fin)
                    link(dve.tensor_reduce(dsum[:, g, 0, :], view(acc_sb[:, g, HD:HD + 1], 0, [[1, HD], [HD, ND - 1]]),
                                           AX_X, ALU.add), s_fin)
                    link(dve.tensor_reduce(dsum[:, g, 1, :], view(pad[:, g, 0, HD - 1:HD], 0,
                                                                  [[1, HD], [2 * HD - 1, ND - 1]]),
                                           AX_X, ALU.add), s_fin)
                    link(dve.tensor_tensor(dsum[:, g, 2, :], dsum[:, g, 0, :], dsum[:, g, 1, :], ALU.add), s_fin)
                    x16 = sums[:, 132 + 18 * g:132 + 18 * g + ND]
                    link(dve.tensor_tensor(dsum[:, g, 0, :].rearrange("p (a i) -> p a i", a=2),
                                           dsum[:, g, 2, :].rearrange("p (a i) -> p a i", a=2),
                                           x16.unsqueeze(1).to_broadcast([128, 2, ND]), ALU.add), s_fin)
                    link(dve.tensor_tensor(acc_sb[:, g, 0:HD], acc_sb[:, g, 0:HD], dsum[:, g, 0, :], ALU.subtract), s_fin)
                    assert n[0] == FIN_ACC[g]
                for g in range(G):
                    x16 = sums[:, 132 + 18 * g:132 + 18 * g + ND]
                    m8 = cst[:, C_M8 + 8 * g:C_M8 + 8 * g + 8]
                    link(dve.tensor_tensor(x5[:, g, :, :], x16.unsqueeze(1).to_broadcast([128, H, ND]),
                                           m8.unsqueeze(2).to_broadcast([128, H, ND]), ALU.mult), s_fin)
                assert n[0] == FIN_X5
                for g in range(G):
                    m4 = cst[:, C_M4:C_M4 + R].unsqueeze(2).to_broadcast([128, R, HD])
                    for to, at, half in ((lin, 1, 1.0), (gram, 1 + HD, 0.5)):
                        s = sums[:, 66 * g + at:66 * g + at + HD].unsqueeze(1).to_broadcast([128, R, HD])
                        o = to[:, g, :].rearrange("p (r d) -> p r d", r=R)
                        dve.scalar_tensor_tensor(out=o, in0=s, scalar=half, in1=m4, op0=ALU.mult,
                                                 op1=ALU.mult).then_inc(s_fin, 1)
                for g in range(G):
                    dve.wait_ge(s_ct, g + 1)
                    dve.tensor_scalar(coef[:, g, :, :].rearrange("p c m -> p (c m)"), p_t[g][:, :], 0.5, None,
                                      ALU.mult).then_inc(s_fin, 1)
                dve.wait_ge(s_ct, G + 1)
                dve.tensor_scalar(coef5[:].rearrange("p g m -> p (g m)"), p_vx[:, 0:G * 128], 0.5, None,
                                  ALU.mult).then_inc(s_fin, 1)
                dve.wait_ge(s_fin, FIN_X5 + 2 * G + G + 1)


def build_b(nc, sem, scope, wprojT, bproj, gate_w, gate_b, consts, table, alr_table, out_v, slots, x_all, q_all, idx_all,
            cst, ident, coef, coef5, lin, gram, sums):
    with scope:
        def sb(name, shape, dt=F32):
            return scope.enter_context(nc.sbuf_tensor(name, shape, dt))

        def ps(name):
            return scope.enter_context(nc.psum_tensor(name, [128, 512], F32))

        sel = sb("sel", [128, 12, 128], F32R)
        wproj = sb("wproj", [128, G, D])
        bproj_t = sb("bproj_t", [PT, D])
        gate_t = sb("gate_t", [128, 2, E])
        gateb_t = sb("gateb_t", [PT, E])
        ones_b = sb("ones_b", [PT, PT])
        row = sb("row", [PT, 4, 2, RW])
        lg = sb("lg", [PT, 2, 4, E])
        lgb, rd, rex, rw = (sb(n, [PT, 2, E]) for n in ("lgb", "rd", "rex", "rw"))
        pm = sb("pm", [PT, 2, E])
        rmax, rsum = sb("rmax", [PT, 2]), sb("rsum", [PT, 2])
        rev_max = sb("rev_max", [PT, 2, 2])
        one_hot = sb("one_hot", [PT, 2, 2, E])
        before = sb("before", [PT, 2, 2, E])
        pos, over, at = sb("pos", [PT, 2]), sb("over", [PT, 2]), sb("at", [PT, 2])
        slot = sb("slot", [PT, 2, 2], I32)
        eps2 = sb("eps2", [PT, 2])
        half2 = sb("half2", [PT, 2])
        q_st = sb("q_st", [PT, 2, 2 * D])
        q_hl = sb("q_hl", [PT, 2, 2 * H, 2, HD], F32R)
        q_hlT = sb("q_hlT", [128, 2, H // 2, NP], F32R)
        q_fT = sb("q_fT", [128, 2, G, NP])
        sq = sb("sq", [128, G, R, CH, NP])
        sq5 = sb("sq5", [128, 2, NP])
        w_t = sb("w_t", [128, 2, G, NP])
        den = sb("den", [128, G, NP])
        y_t = sb("y_t", [128, G, NP])
        idx = sb("idx", [PT, 2, 2, 2], I32)
        rows = sb("rows", [PT, 2, 2, TW])
        alr_g = sb("alr_g", [PT, 2, 2, 2 * GH])
        ga, gl, gs, ge, gp = (sb(n, [PT, 2, GH]) for n in ("ga", "gl", "gs", "ge", "gp"))
        gmax, gsum, grec = sb("gmax", [PT, 2]), sb("gsum", [PT, 2]), sb("grec", [PT, 2])
        prod = sb("prod", [PT, 2, GH, GD])
        tmp = sb("tmp", [PT, 2, 2, GD])
        st2 = sb("st2", [PT, 2, 6])
        ve2 = sb("ve2", [PT, 2, 2])
        x_st = sb("x_st", [PT, 2, 2, D])
        x_T = sb("x_T", [128, 2, NP])
        sel_raw = sq[:].rearrange("p g r c n -> p (g r c n)")[:, 0:12 * 128].rearrange("p (s m) -> p s m", s=12)

        p_sel = [ps(f"p_sel{i}") for i in range(3)]
        p_y = [ps("p_y0"), ps("p_y1")]
        p_gram, p_tr, p_proj = ps("p_gram"), ps("p_tr"), ps("p_proj")

        b_ld, b_ini, b_sel = sem("b_ld"), sem("b_ini"), sem("b_sel")
        b_met = [sem("b_met_pool"), sem("b_met_dve"), sem("b_met_act")]
        s_qst, s_qhi, s_qlo = sem("s_qst"), sem("s_qhi"), sem("s_qlo")
        s_trh, s_trf, s_trx = sem("s_trh"), sem("s_trf"), sem("s_trx")
        s_evh, s_evf, s_evx = sem("s_evh"), sem("s_evf"), sem("s_evx")
        s_fill, s_sqd = sem("s_fill"), sem("s_sqd")
        s_gram, s_w2 = sem("s_gram"), sem("s_w2")
        s_yn = [sem("s_yn0"), sem("s_yn1")]
        s_den, s_rden, s_y = ([sem(f"{n}{g}") for g in range(G)] for n in ("s_den", "s_rden", "s_y"))
        s_proj, s_x2, s_st2, s_mv2, s_ve2, s_rs2 = (sem(n) for n in ("s_proj", "s_x2", "s_st2", "s_mv2", "s_ve2",
                                                                     "s_rs2"))
        s_xst, s_gate, s_gev = sem("s_xst"), sem("s_gate"), sem("s_gev")
        s_route, s_rd, s_rex, s_oh, s_gt = sem("s_route"), sem("s_rd"), sem("s_rex"), sem("s_oh"), sem("s_gt")
        s_lgb, s_rmax, s_rw, s_rev, s_hot, s_rsum = (sem(n) for n in ("s_lgb", "s_rmax", "s_rw", "s_rev", "s_hot",
                                                                      "s_rsum"))
        s_pos, s_slot = sem("s_pos"), sem("s_slot")
        s_scat, s_out = ([sem(f"{n}{i}") for i in range(4)] for n in ("s_scat", "s_out"))
        s_idx, s_g = sem("s_idx"), [sem("s_g0"), sem("s_g1")]
        s_ga, s_gl, s_gmax, s_gs, s_ge, s_gsum, s_grec, s_gp, s_prod, s_tmp = (
            sem(n) for n in ("s_ga", "s_gl", "s_gmax", "s_gs", "s_ge", "s_gsum", "s_grec", "s_gp", "s_prod", "s_tmp"))
        s_xb, s_gadd = sem("s_xb"), sem("s_gadd")
        FILLS = 17
        LOADS = 5 * 16

        def run(eng, first, last, step):
            pipeline(eng, first, last, 7, 23, step, turn=4)

        def gate_and_positions(j):
            return 0 if inside(j - 3, TILES // 2) else 2, 4 if inside(j - 4, TILES // 2) else 2

        with nc.Block() as block:
            @block.sync
            def _(sp):
                sp.dma_start(sel_raw, consts[:, C_SEL:NC_].rearrange("p (s m) -> p s m", s=12)).then_inc(b_ld, 16)
                sp.dma_start(wproj[:], wprojT.rearrange("(g p) n -> p g n", p=128)).then_inc(b_ld, 16)
                sp.dma_start(bproj_t[:], bproj.partition_broadcast(PT)).then_inc(b_ld, 16)
                sp.dma_start(gate_t[:], gate_w.rearrange("(k p) n -> p k n", p=128)).then_inc(b_ld, 16)
                sp.dma_start(gateb_t[:], gate_b.partition_broadcast(PT)).then_inc(b_ld, 16)

                def step(j, r, div):
                    sp.wait_ge(s_x2, j)
                    sp.dma_start(out_v[:, bass.ds(j * 2 - 2, 2), :], row[:, (r - 1) % 4, :, 0:D]
                                 ).then_inc(s_out[(r - 1) % 4], 16)
                run(sp, 1, TILES // 2 + 1, step)
                for i in range(4):
                    sp.wait_ge(s_out[i], 16 * len(range(i, TILES // 2, 4)))

            @block.gpsimd
            def _(pool):
                pool.memset(eps2[:], LN_EPS).then_inc(b_ini, 1)
                pool.memset(half2[:], -0.5).then_inc(b_ini, 1)
                pool.memset(ones_b[:], 1.0).then_inc(b_ini, 1)
                pool.memset(one_hot[:], 0.0).then_inc(b_ini, 1)
                pool.memset(before[:], 0.0).then_inc(b_ini, 1)
                pool.wait_ge(b_ini, 5)
                pool.wait_ge(b_ld, LOADS)

                def step(j, r, div):
                    p = r % 2
                    if inside(j, TILES // 2):
                        xj = x_all[:, bass.ds(j * 2, 2), :]
                        pool.tensor_tensor(xj, xj, bproj_t[:].unsqueeze(1).to_broadcast([PT, 2, D]),
                                           ALU.add).then_inc(s_xb, 1)
                    if inside(j - 5, TILES // 2):
                        pool.wait_ge(s_slot, j - 4)
                        pool.wait_ge(s_gt, j - 4)
                        pool.sem_inc(b_met[0], 1)
                        for u in range(2):
                            pool.indirect_dma_start(
                                slots, bass.IndirectOffsetOnAxis(ap=slot[:, 1 - p, u:u + 1], axis=0),
                                row[:, (r - 5) % 4, u, :], None, bounds_check=E * SLOTS - 1,
                                oob_is_err=False).then_inc(s_scat[(r - 5) % 4], 16)
                    if inside(j - 1, TILES // 2):
                        pool.wait_ge(s_mv2, 2 * j)
                        pool.tensor_tensor(ve2[:, 1 - p, :], row[:, (r - 1) % 4, :, VAR], eps2[:],
                                           ALU.add).then_inc(s_ve2, 1)
                        pool.wait_ge(s_ve2, j)
                        pool.tensor_tensor(row[:, (r - 1) % 4, :, RSTD], ve2[:, 1 - p, :], half2[:],
                                           ALU.pow).then_inc(s_rs2, 1)
                    s = j + 2
                    if inside(s, TILES // 2):
                        wait(pool, s_g[p], 64 * (div(0, 2) + 1))
                        wait(pool, s_tmp, j + 1)
                        pool.sem_inc(b_met[0], 1)
                        pool.tensor_copy(idx[:, p, :, :], idx_all[:, :, bass.ds(j * 2 + 4, 2)]).then_inc(s_idx, 1)
                        pool.wait_ge(s_idx, j + 3)
                        pool.sem_inc(b_met[0], 1)
                        for u in range(2):
                            pool.indirect_dma_start(
                                rows[:, p, u, :], None, table,
                                bass.IndirectOffsetOnAxis(ap=idx[:, p, 1, u:u + 1], axis=0)).then_inc(s_g[p], 16)
                            pool.indirect_dma_start(
                                alr_g[:, p, u, :], None, alr_table,
                                bass.IndirectOffsetOnAxis(ap=idx[:, p, 0, u:u + 1], axis=0)).then_inc(s_g[p], 16)
                    if inside(j, TILES // 2):
                        pool.wait_ge(s_xb, j + 1)
                        pool.wait_ge(s_tmp, j + 1)
                        pool.sem_inc(b_met[0], 1)
                        x4 = xj.rearrange("p t (r d) -> p t r d", r=GH)
                        pool.tensor_tensor(x4, x4, tmp[:, p, :, :].unsqueeze(2).to_broadcast([PT, 2, GH, GD]),
                                           ALU.add).then_inc(s_gadd, 1)
                run(pool, -2, TILES // 2 + 5, step)
                for i in range(4):
                    pool.wait_ge(s_scat[i], 32 * len(range(i, TILES // 2, 4)))

            @block.scalar
            def _(act):
                act.wait_ge(b_ld, LOADS)
                act.activation(sel[:], sel_raw, ACT.Copy).then_inc(b_sel, 1)
                act.wait_ge(b_sel, 1)

                def square(j, p, k):
                    act.wait_ge(s_fill, j * FILLS + k + 1)
                    if k == 8:
                        o, n = sq5[:, p, :], NP
                    else:
                        g, f = k // 9, k % 9
                        o = sq[:, g, f % 4, 2 * (f // 4):2 * (f // 4) + 2, :].rearrange("p c n -> p (c n)")
                        n = 2 * NP
                    act.activation(o, p_sel[k % 3][:, 0:n], ACT.Square).then_inc(s_sqd, 1)

                def step(j, r, div):
                    p = r % 2
                    main, nxt = inside(j, TILES // 2), inside(j + 1, TILES // 2)
                    for k in range(FILLS):
                        if main:
                            square(j, p, k)
                        if k == 2 and inside(j + 2, TILES // 2):
                            act.wait_ge(s_qst, j + 3)
                            wait(act, s_trh, 2 * (j + 1))
                            wait(act, s_qlo, j + 1)
                            act.activation(q_hl[:, p, :, 0, :], q_st[:, p, :].rearrange("p (h d) -> p h d", d=HD),
                                           ACT.Copy).then_inc(s_qhi, 1)
                        if nxt and k in (5, 8):
                            b = 2 * (k // 8)
                            act.wait_ge(s_trh, 2 * (j + 1) + k // 8 + 1)
                            act.activation(q_hlT[:, 1 - p, b:b + 2, :].rearrange("p b n -> p (b n)"),
                                           p_tr[:, 0:2 * NP], ACT.Copy).then_inc(s_evh, 1)
                        if main and k == 5:
                            act.wait_ge(s_gs, j + 1)
                            wait(act, s_gp, j)
                            act.activation(ge[:], gs[:], ACT.Exp).then_inc(s_ge, 1)
                        if k == 9 and inside(j - 4, TILES // 2):
                            act.wait_ge(s_rd, j - 3)
                            wait(act, s_gt, j - 4)
                            act.activation(rex[:], rd[:], ACT.Exp).then_inc(s_rex, 1)
                        if nxt and k == 12:
                            act.wait_ge(s_trf, j + 2)
                            wait(act, s_w2, 2 * j)
                            act.activation(q_fT[:, 1 - p, :, :].rearrange("p g n -> p (g n)"), p_tr[:, 0:2 * NP],
                                           ACT.Copy).then_inc(s_evf, 1)
                        a, b = gate_and_positions(j)
                        if k == 15 and a < b:
                            act.wait_ge(s_gate, j - 2)
                            wait(act, s_lgb, j - 4)
                            act.activation(lg[:, p, a:b, :].rearrange("p t e -> p (t e)"), p_tr[0:PT, a * E:b * E],
                                           ACT.Copy).then_inc(s_gev, 1)
                        if k == 16 and inside(j - 2, TILES // 2):
                            act.wait_ge(s_trx, j - 1)
                            act.activation(x_T[:].rearrange("p k n -> p (k n)"), p_tr[:, 0:2 * NP],
                                           ACT.Copy).then_inc(s_evx, 1)
                run(act, -2, TILES // 2 + 4, step)

            @block.tensor
            def _(pe):
                pe.wait_ge(b_sel, 1)
                pe.wait_ge(b_ini, 5)
                pe.wait_ge(b_ld, LOADS)

                def fill(j, p, k):
                    if k == 0:
                        pe.wait_ge(s_evh, 2 * (j + 1))
                    if k >= 3:
                        pe.wait_ge(s_sqd, j * FILLS + k - 2)
                    else:
                        wait(pe, s_sqd, (j - 1) * FILLS + (16, 17, 15)[k])
                    bank = p_sel[k % 3]
                    if k == 8:
                        for b in range(H // 2):
                            mm = pe.matmul(bank[:, 0:NP], sel[:, 8 + b, :], q_hlT[:, p, b, :], start=b == 0,
                                           stop=b == H // 2 - 1)
                    else:
                        g, f = k // 9, k % 9
                        head = R * g + f % 4
                        for c in range(2):
                            ch = 2 * (f // 4) + c
                            mm = pe.matmul(bank[:, c * NP:(c + 1) * NP], sel[:, (head % 2) * CH + ch, :],
                                           q_hlT[:, p, head // 2, :], start=True, stop=True)
                    mm.then_inc(s_fill, 1)

                def contract(g, j, c):
                    pe.wait_ge(s_sqd, j * FILLS + 9 * g + 4 * (c // 2) + 4)
                    if c == 0:
                        wait(pe, s_y[g], j)
                    for r in range(R):
                        q = slice(HD * r, HD * r + HD)
                        pe.matmul(p_y[g][q, 0:NP], coef[:, g, c, q], sq[:, g, r, c, :], start=c == 0,
                                  stop=False, skip_group_check=True)

                def finish(g, j, p):
                    pe.wait_ge(s_sqd, j * FILLS + 9)
                    pe.matmul(p_y[g][:, 0:NP], coef5[:, g, :], sq5[:, p, :], start=False, stop=False,
                              skip_group_check=True)
                    pe.matmul(p_y[g][:, 0:NP], lin[:, g, :], q_fT[:, p, g, :], start=False, stop=True,
                              skip_group_check=True)

                def spread_norm(g, j, p):
                    pe.wait_ge(s_w2, 2 * j + g + 1)
                    pe.matmul(p_y[g][:, NP:2 * NP], cst[:, C_BLK:C_BLK + 128], w_t[:, p, g, :], start=True,
                              stop=True, skip_group_check=True).then_inc(s_yn[g], 1)

                def turn_hl(j, p, i):
                    pe.wait_ge(s_qhi, j + 1)
                    pe.wait_ge(s_qlo, j + 1)
                    if i == 0:
                        wait(pe, s_evx, j - 3)
                    else:
                        pe.wait_ge(s_evh, 2 * j + 1)
                    for b in range(2):
                        for u in range(2):
                            hh = 2 * (2 * i + b)
                            mm = pe.transpose(
                                p_tr[:, b * NP + u * PT:b * NP + (u + 1) * PT],
                                q_hl[:, p, u * H + hh:u * H + hh + 2, :, :].rearrange("p h w d -> p (h w d)").bitcast(F32),
                                ident[0:PT, 0:PT])
                    mm.then_inc(s_trh, 1)

                def project(j, u):
                    if u == 0:
                        pe.wait_ge(s_y[0], j + 1)
                        pe.wait_ge(s_y[1], j + 1)
                        wait(pe, s_x2, j)
                    for g in range(G):
                        mm = pe.matmul(p_proj[0:PT, u * D:(u + 1) * D], y_t[:, g, u * PT:(u + 1) * PT], wproj[:, g, :],
                                       start=g == 0, stop=g == G - 1)
                    if u == 1:
                        mm.then_inc(s_proj, 1)

                def step(j, r, div):
                    p = r % 2
                    main, nxt, prev = (inside(j + d, TILES // 2) for d in (0, 1, -1))
                    for k in range(FILLS):
                        if main:
                            fill(j, p, k)
                        if prev:
                            if k == 0:
                                finish(1, j - 1, 1 - p)
                            if k in (1, 2):
                                contract(1, j - 1, k + 1)
                            if k == 3:
                                spread_norm(1, j - 1, 1 - p)
                            if k in (9, 10):
                                project(j - 1, k - 9)
                        if nxt:
                            if k in (4, 7):
                                turn_hl(j + 1, 1 - p, k // 7)
                            if k == 11:
                                pe.wait_ge(s_qst, j + 2)
                                pe.wait_ge(s_evh, 2 * (j + 2))
                                for g in range(G):
                                    for u in range(2):
                                        mm = pe.transpose(p_tr[:, g * NP + u * PT:g * NP + (u + 1) * PT],
                                                          q_st[:, 1 - p, u * D + g * 128:u * D + (g + 1) * 128],
                                                          ident[0:PT, 0:PT])
                                mm.then_inc(s_trf, 1)
                        if main:
                            if k in (5, 6):
                                contract(0, j, k - 5)
                            if k == 8:
                                pe.wait_ge(s_evf, j + 1)
                                wait(pe, s_w2, 2 * j)
                                for g in range(G):
                                    mm = pe.matmul(p_gram[:, g * NP:(g + 1) * NP], gram[:, g, :], q_fT[:, p, g, :],
                                                   start=True, stop=True)
                                mm.then_inc(s_gram, 1)
                            if k in (10, 11):
                                contract(0, j, k - 8)
                            if k == 12:
                                finish(0, j, p)
                            if k == 13:
                                spread_norm(0, j, p)
                            if k in (15, 16):
                                contract(1, j, k - 15)
                        if k == 14:
                            gate_step(j, p)
                        if k == 16 and inside(j - 2, TILES // 2):
                            pe.wait_ge(s_xst, 2 * (j - 1))
                            wait(pe, s_gev, j - 2)
                            if isinstance(j, int):
                                wait(pe, s_evf, min(j + 2, TILES // 2))
                            for q in range(2):
                                for u in range(2):
                                    mm = pe.transpose(p_tr[:, q * NP + u * PT:q * NP + (u + 1) * PT],
                                                      x_st[:, p, u, q * 128:(q + 1) * 128], ident[0:PT, 0:PT])
                            mm.then_inc(s_trx, 1)

                def gate_step(j, p):
                    a, b = gate_and_positions(j)
                    if a == b:
                        return
                    if isinstance(j, int):
                        wait(pe, s_evf, min(j + 2, TILES // 2))
                    else:
                        pe.wait_ge(s_evf, j + 2)
                    if a == 0:
                        pe.wait_ge(s_evx, j - 2)
                        for u in range(2):
                            for q in range(2):
                                mm = pe.matmul(p_tr[0:PT, u * E:(u + 1) * E], x_T[:, q, u * PT:(u + 1) * PT],
                                               gate_t[:, q, :], start=q == 0, stop=q == 1)
                    if b == 4:
                        pe.wait_ge(s_oh, j - 3)
                        pe.matmul(p_tr[0:PT, 2 * E:4 * E], cst[0:PT, C_TRI:C_TRI + PT],
                                  one_hot[:, p, :, :].rearrange("p u e -> p (u e)"), start=True, stop=False)
                        mm = pe.matmul(p_tr[0:PT, 2 * E:4 * E], ones_b[:],
                                       before[:, p, :, :].rearrange("p u e -> p (u e)"), start=False, stop=True)
                    mm.then_inc(s_gate, 1)
                run(pe, -1, TILES // 2 + 4, step)

            @block.vector
            def _(dve):
                dve.wait_ge(b_ini, 5)
                dve.wait_ge(b_ld, LOADS)

                STEPS = 3

                def output(g, j, p):
                    dve.wait_ge(s_yn[g], j + 1)
                    wait(dve, s_y[g], j)
                    dve.tensor_scalar(den[:, g, :], p_y[g][:, NP:2 * NP], float(N), None, ALU.add).then_inc(s_den[g], 1)
                    dve.wait_ge(s_den[g], j + 1)
                    dve.reciprocal(den[:, g, :], den[:, g, :]).then_inc(s_rden[g], 1)
                    dve.wait_ge(s_rden[g], j + 1)
                    wait(dve, s_proj, j)
                    c = 132 + 18 * g + ND
                    dve.scalar_tensor_tensor(out=y_t[:, g, :], in0=p_y[g][:, 0:NP], scalar=sums[:, c:c + 1],
                                             in1=den[:, g, :], op0=ALU.add, op1=ALU.mult).then_inc(s_y[g], 1)

                def step(j, r, div):
                    p = r % 2
                    if inside(j - 2, TILES // 2):
                        dve.wait_ge(s_rs2, j - 1)
                        wait(dve, s_trx, j - 3)
                        for u in range(2):
                            a = row[:, (r - 2) % 4, u, :]
                            dve.tensor_scalar(x_st[:, p, u, :], a[:, 0:D], a[:, MEAN:MEAN + 1], a[:, RSTD:RSTD + 1],
                                              ALU.subtract, ALU.mult).then_inc(s_xst, 1)
                    if inside(j + 2, TILES // 2):
                        wait(dve, s_trf, j + 1)
                        wait(dve, s_qhi, j + 1)
                        wait(dve, s_qlo, j + 1)
                        dve.tensor_copy(q_st[:, p, :], q_all[:, bass.ds(j * 2 + 4, 2), :].rearrange("p t d -> p (t d)")
                                        ).then_inc(s_qst, 1)
                    if inside(j - 5, TILES // 2):
                        dve.wait_ge(s_gev, j - 3)
                        dve.tensor_tensor(pm[:], lg[:, 1 - p, 2:4, :], one_hot[:, 1 - p, :, :], ALU.mult
                                          ).then_inc(s_route, 1)
                        dve.wait_ge(s_route, STEPS * (j - 5) + 1)
                        dve.tensor_reduce(pos[:], pm[:], AX_X, ALU.add).then_inc(s_pos, 1)
                        dve.wait_ge(s_pos, j - 4)
                        dve.tensor_scalar(over[:], pos[:], float(CAP), NO_TOKEN, ALU.is_gt, ALU.mult).then_inc(s_route, 1)
                        dve.scalar_tensor_tensor(out=at[:], in0=rev_max[:, 1 - p, :], scalar=-float(SLOTS), in1=pos[:],
                                                 op0=ALU.mult, op1=ALU.add).then_inc(s_route, 1)
                        dve.wait_ge(s_route, STEPS * (j - 5) + 3)
                        wait(dve, s_scat[(r - 7) % 4], 32 * div(-3, 4))
                        dve.scalar_tensor_tensor(out=slot[:, 1 - p, :], in0=at[:], scalar=float(E * SLOTS - 1),
                                                 in1=over[:], op0=ALU.add, op1=ALU.add).then_inc(s_slot, 1)
                    if inside(j - 4, TILES // 2):
                        rev = cst[0:PT, C_REV:C_REV + E].unsqueeze(1).to_broadcast([PT, 2, E])
                        dve.wait_ge(s_gev, j - 3)
                        dve.tensor_tensor(lgb[:], lg[:, 1 - p, 0:2, :], gateb_t[:].unsqueeze(1).to_broadcast([PT, 2, E]),
                                          ALU.add).then_inc(s_lgb, 1)
                        dve.wait_ge(s_lgb, j - 3)
                        dve.tensor_reduce(rmax[:], lgb[:], AX_X, ALU.max).then_inc(s_rmax, 1)
                        dve.wait_ge(s_rmax, j - 3)
                        wait(dve, s_rex, j - 4)
                        dve.tensor_tensor(rd[:], lgb[:], rmax[:].unsqueeze(2).to_broadcast([PT, 2, E]),
                                          ALU.subtract).then_inc(s_rd, 1)
                        dve.wait_ge(s_rd, j - 3)
                        dve.scalar_tensor_tensor(out=rw[:], in0=rd[:], scalar=0.0, in1=rev, op0=ALU.is_equal,
                                                 op1=ALU.mult).then_inc(s_rw, 1)
                        dve.wait_ge(s_rw, j - 3)
                        dve.tensor_reduce(rev_max[:, p, :], rw[:], AX_X, ALU.max).then_inc(s_rev, 1)
                        dve.wait_ge(s_rev, j - 3)
                        dve.tensor_tensor(one_hot[:, p, :, :], rev, rev_max[:, p, :].unsqueeze(2).to_broadcast([PT, 2, E]),
                                          ALU.is_equal).then_inc(s_hot, 1)
                        dve.tensor_tensor(before[:, p, 0, :], before[:, 1 - p, 1, :], one_hot[:, 1 - p, 1, :],
                                          ALU.add).then_inc(s_hot, 1)
                        dve.wait_ge(s_hot, 2 * (j - 3))
                        dve.tensor_tensor(before[:, p, 1, :], before[:, p, 0, :], one_hot[:, p, 0, :],
                                          ALU.add).then_inc(s_oh, 1)
                    if inside(j, TILES // 2):
                        dve.wait_ge(s_g[p], 64 * (div(0, 2) + 1))
                        dve.tensor_tensor(ga[:], rows[:, p, :, D:TW], alr_g[:, p, :, GH:2 * GH], ALU.add).then_inc(s_ga, 1)
                        dve.wait_ge(s_ga, j + 1)
                        dve.scalar_tensor_tensor(out=gl[:], in0=ga[:], scalar=0.01, in1=ga[:], op0=ALU.mult,
                                                 op1=ALU.max).then_inc(s_gl, 1)
                        dve.wait_ge(s_gl, j + 1)
                        dve.tensor_reduce(gmax[:], gl[:], AX_X, ALU.max).then_inc(s_gmax, 1)
                        dve.wait_ge(s_gmax, j + 1)
                        wait(dve, s_ge, j)
                        dve.tensor_tensor(gs[:], gl[:], gmax[:].unsqueeze(2).to_broadcast([PT, 2, GH]),
                                          ALU.subtract).then_inc(s_gs, 1)
                    if inside(j - 1, TILES // 2):
                        output(1, j - 1, 1 - p)
                    if inside(j + 2, TILES // 2):
                        dve.wait_ge(s_qhi, j + 3)
                        wait(dve, s_trh, 2 * (j + 1))
                        dve.tensor_tensor(q_hl[:, p, :, 1, :], q_st[:, p, :].rearrange("p (h d) -> p h d", d=HD),
                                          q_hl[:, p, :, 0, :].bitcast(F32), ALU.subtract).then_inc(s_qlo, 1)
                    if inside(j, TILES // 2):
                        dve.wait_ge(s_gram, j + 1)
                        wait(dve, s_yn[1], j - 1)
                        for g in range(G):
                            dve.scalar_tensor_tensor(out=w_t[:, p, g, :], in0=p_gram[:, g * NP:(g + 1) * NP],
                                                     scalar=sums[:, 66 * g:66 * g + 1], in1=q_fT[:, p, g, :],
                                                     op0=ALU.add, op1=ALU.mult).then_inc(s_w2, 1)
                    if inside(j, TILES // 2):
                        dve.wait_ge(s_ge, j + 1)
                        dve.tensor_reduce(gsum[:], ge[:], AX_X, ALU.add).then_inc(s_gsum, 1)
                        dve.wait_ge(s_gsum, j + 1)
                        dve.reciprocal(grec[:], gsum[:]).then_inc(s_grec, 1)
                        dve.wait_ge(s_grec, j + 1)
                        dve.tensor_tensor(gp[:], ge[:], grec[:].unsqueeze(2).to_broadcast([PT, 2, GH]),
                                          ALU.mult).then_inc(s_gp, 1)
                        dve.wait_ge(s_gp, j + 1)
                        dve.tensor_tensor(prod[:], rows[:, p, :, 0:D].rearrange("p t (h d) -> p t h d", h=GH),
                                          gp[:].unsqueeze(3).to_broadcast([PT, 2, GH, GD]), ALU.mult).then_inc(s_prod, 1)
                        dve.wait_ge(s_prod, j + 1)
                        wait(dve, s_gadd, j - 1)
                        dve.tensor_reduce(tmp[:, p, :, :], prod[:].rearrange("p t h d -> p t d h"), AX_X,
                                          ALU.add).then_inc(s_tmp, 1)
                    if inside(j - 1, TILES // 2):
                        dve.wait_ge(s_proj, j)
                        dve.wait_ge(s_gadd, j)
                        wait(dve, s_scat[(r - 1) % 4], 32 * div(-1, 4))
                        wait(dve, s_out[(r - 1) % 4], 16 * div(-1, 4))
                        dve.tensor_tensor(row[:, (r - 1) % 4, :, 0:D], p_proj[0:PT, :].rearrange("p (t d) -> p t d", t=2),
                                          x_all[:, bass.ds(j * 2 - 2, 2), :], ALU.add).then_inc(s_x2, 1)
                        dve.wait_ge(s_x2, j)
                        wait(dve, s_mv2, 2 * (j - 1))
                        dve.sem_inc(b_met[1], 1)
                        for u in range(2):
                            dve.bn_stats(st2[:, u, :], row[:, (r - 1) % 4, u, 0:D]).then_inc(s_st2, 1)
                        dve.wait_ge(s_st2, 2 * j)
                        dve.sem_inc(b_met[1], 1)
                        for u in range(2):
                            dve.bn_aggr(row[:, (r - 1) % 4, u, MEAN:VAR + 1], st2[:, u, :]).then_inc(s_mv2, 1)
                    if inside(j - 4, TILES // 2):
                        dve.wait_ge(s_rex, j - 3)
                        dve.tensor_reduce(rsum[:], rex[:], AX_X, ALU.add).then_inc(s_rsum, 1)
                        dve.tensor_scalar(row[:, (r - 4) % 4, :, TOKEN], cst[0:PT, bass.ds(j * 2 + (C_TOK - 8), 2)], 1.0,
                                          None, ALU.mult).then_inc(s_rsum, 1)
                        dve.wait_ge(s_rsum, 2 * (j - 3))
                        dve.reciprocal(row[:, (r - 4) % 4, :, GATE], rsum[:]).then_inc(s_gt, 1)
                    if inside(j, TILES // 2):
                        output(0, j, p)
                run(dve, -2, TILES // 2 + 5, step)


def build_experts(nc, sem, scope, w1, b1, w2, b2, slots, out, ident):
    with scope:
        def sb(name, shape, dt=F32):
            return scope.enter_context(nc.sbuf_tensor(name, shape, dt))

        def ps(name):
            return scope.enter_context(nc.psum_tensor(name, [128, 512], F32))

        BI = SI // 2
        w1_raw, w2_raw = sb("w1_raw", [128, 2, F]), sb("w2_raw", [128, FC, D])
        w1_hi, w1_lo = sb("w1_hi", [128, 2, 2, F], F32R), sb("w1_lo", [128, 2, 2, F], F32R)
        w2_hi, w2_lo = sb("w2_hi", [128, 2, FC, D], F32R), sb("w2_lo", [128, 2, FC, D], F32R)
        b1_rows, b1_T, b1_now = sb("b1_rows", [E * FC, 128]), sb("b1_T", [128, E * FC]), sb("b1_now", [128, 2, FC])
        b2_all = sb("b2_all", [SP_, E, D])
        rows = sb("slot_rows", [SP_, 4, BI, RW])
        token = sb("token", [SP_, 4, BI], I32)
        xn = sb("xn_e", [SP_, BI, D])
        xT_hi, xT_lo = sb("xTe_hi", [128, 2, 2, HALF], F32R), sb("xTe_lo", [128, 2, 2, HALF], F32R)
        h32 = sb("h32", [128, 4, HALF])
        h_hi, h_lo = sb("h_hi", [128, 4, HALF], F32R), sb("h_lo", [128, 4, HALF], F32R)
        yb, z, big, fin, alt = (sb(n, [SP_, BI * D]) for n in ("yb", "z", "big", "fin", "alt"))
        res = sb("res", [SP_, 2, BI, D])

        p_h = [ps("p_h0"), ps("p_h1")]
        p_x = [ps("p_x0"), ps("p_x1")]
        p_o = [[ps(f"p_o{b}{i}") for i in range(2)] for b in range(2)]

        e_ld, e_b1t, e_b1 = sem("e_ld"), sem("e_b1t"), sem("e_b1")
        e_met = [sem("e_met_pool"), sem("e_met_dve")]
        s_w1ld, s_w2ld, s_rows = sem("s_w1ld"), sem("s_w2ld"), [sem(f"e_rows{i}") for i in range(4)]
        s_whi, s_wlo, s_b1 = sem("e_whi"), sem("e_wlo"), sem("s_b1")
        s_xn, s_tok, s_tr, s_xhi, s_xlo = sem("e_xn"), sem("s_tok"), sem("s_tr"), sem("s_xhi"), sem("s_xlo")
        s_hmm, s_h32, s_hhi, s_hlo, s_ymm = sem("s_hmm"), sem("s_h32"), sem("s_hhi"), sem("s_hlo"), sem("s_ymm")
        s_yb, s_z, s_cmp, s_alt, s_alt2, s_sel, s_res, e_b2 = (
            sem(n) for n in ("s_yb", "s_z", "s_cmp", "s_alt", "s_alt2", "s_selz", "s_res", "e_b2"))
        s_put = [sem("s_put0"), sem("s_put1")]
        FLT_MAX = float(np.finfo(np.float32).max)
        PIECES = 2 * BI

        def run(eng, first, last, step):
            pipeline(eng, first, last, 2, 6, step)

        def piece(w_1, w_2, c, *slot):
            a = w_1[(slice(None), *slot)] if slot else w_1[:]
            b = w_2[(slice(None), *slot)] if slot else w_2[:]
            a = a.rearrange("p k f -> p (k f)") if c < BI else b.rearrange("p c d -> p (c d)")
            return a[:, (c % BI) * 512:(c % BI) * 512 + 512]

        with nc.Block() as block:
            @block.sync
            def _(sp):
                sp.dma_start(b1_rows[:], b1.rearrange("e (c m) -> (e c) m", m=128)).then_inc(e_ld, 16)

                def step(e, p, div):
                    if inside(e + 1, E):
                        wait(sp, s_wlo, PIECES * (e + 1))
                        sp.dma_start(w1_raw[:], w1[bass.ds(e + 1, 1), :, :].rearrange("o (k p) f -> p (o k) f", p=128)
                                     ).then_inc(s_w1ld, 16)
                        for b in range(2):
                            wait(sp, s_res, 2 * (e - 1) + b + 1)
                            wait(sp, s_tok, 2 * (e - 1) + b + 1)
                            sp.dma_start(rows[:, 2 * (1 - p) + b, :, :],
                                         slots[bass.ds(e * SLOTS + SLOTS, SLOTS), :]
                                         .rearrange("(p i) d -> p i d", i=SI)[:, b * BI:(b + 1) * BI, :]
                                         ).then_inc(s_rows[2 * (1 - p) + b], 16)
                        sp.dma_start(w2_raw[:], w2[bass.ds(e + 1, 1), :, :].rearrange("o (c p) d -> p (o c) d", p=128)
                                     ).then_inc(s_w2ld, 16)
                        if isinstance(e, int) and e == -1:
                            sp.dma_start(b2_all[:].rearrange("p e d -> p (e d)"),
                                         b2.rearrange("e d -> (e d)").partition_broadcast(SP_)).then_inc(e_b2, 16)
                run(sp, -1, E, step)
                sp.wait_ge(e_b2, 16)

            @block.gpsimd
            def _(pool):
                def step(e, p, div):
                    for b in range(2):
                        s = e * 2 + b
                        for c in range(FC):
                            k = e * 2 * FC + (b * FC + c)
                            if c == 1 and inside(s - 2, 2 * E):
                                pool.wait_ge(s_res, s - 1)
                                pool.sem_inc(e_met[0], 1)
                                for i in range(BI):
                                    pool.indirect_dma_start(
                                        out, bass.IndirectOffsetOnAxis(ap=token[:, (2 * p + b - 2) % 4, i:i + 1], axis=0),
                                        res[:, b, i, :], None, bounds_check=N - 1, oob_is_err=False).then_inc(s_put[b], 16)
                run(pool, 0, E + 1, step)
                for b in range(2):
                    pool.wait_ge(s_put[b], 16 * BI * E)

            @block.scalar
            def _(act):
                act.wait_ge(e_b1t, 1)
                act.activation(b1_T[:], p_h[0][:, 0:E * FC], ACT.Copy).then_inc(e_b1, 1)

                def step(e, p, div):
                    for b in range(2):
                        s = e * 2 + b
                        for c in range(FC):
                            k = e * 2 * FC + (b * FC + c)
                            if inside(e, E):
                                if b == 0 and c == 0:
                                    act.wait_ge(s_b1, e + 1)
                                act.wait_ge(s_hmm, k + 1)
                                wait(act, s_hlo, k - 3)
                                act.activation(h32[:, c % 4, :], p_h[c % 2][:, 0:HALF], ACT.Relu,
                                               bias=b1_now[:, p, c:c + 1]).then_inc(s_h32, 1)
                                act.wait_ge(s_h32, k + 1)
                                wait(act, s_ymm, k - 3)
                                act.activation(h_hi[:, c % 4, :], h32[:, c % 4, :], ACT.Copy).then_inc(s_hhi, 1)
                            if c == 6 and inside(s - 1, 2 * E):
                                act.wait_ge(s_alt, s)
                                act.activation(alt[:], alt[:], ACT.Copy, scale=-10000.0).then_inc(s_alt2, 1)
                            if c in (4, 5) and inside(s + 1, 2 * E):
                                act.wait_ge(s_tr, 2 * (s + 1) + c - 3)
                                wait(act, s_hmm, FC * s)
                                act.activation(xT_hi[:, 1 - b, c - 4, :], p_x[c - 4][:, 0:HALF],
                                               ACT.Copy).then_inc(s_xhi, 1)
                            if b == 1 and inside(e + 1, E):
                                if c == 0:
                                    act.wait_ge(s_w1ld, 16 * (e + 2))
                                    wait(act, s_hmm, 2 * FC * e)
                                if c == BI:
                                    act.wait_ge(s_w2ld, 16 * (e + 2))
                                    wait(act, s_ymm, 2 * FC * e)
                                act.activation(piece(w1_hi, w2_hi, c, 1 - p), piece(w1_raw, w2_raw, c),
                                               ACT.Copy).then_inc(s_whi, 1)
                            if c == 2 and inside(s - 1, 2 * E):
                                act.wait_ge(s_yb, 2 * s)
                                wait(act, s_sel, s - 1)
                                for i in range(BI):
                                    act.activation(z[:, i * D:(i + 1) * D], yb[:, i * D:(i + 1) * D], ACT.Copy,
                                                   scale=rows[:, (2 * p + b - 1) % 4, i, GATE:GATE + 1]).then_inc(s_z, 1)
                run(act, -1, E + 1, step)

            @block.tensor
            def _(pe):
                pe.wait_ge(e_ld, 16)
                pe.transpose(p_h[0][:, 0:E * FC], b1_rows[:], ident[0:E * FC, 0:E * FC]).then_inc(e_b1t, 1)
                pe.wait_ge(e_b1, 1)

                def step(e, p, div):
                    for b in range(2):
                        s = e * 2 + b
                        for c in range(FC):
                            k = e * 2 * FC + (b * FC + c)
                            if inside(e, E):
                                if c == 0:
                                    pe.wait_ge(s_xlo, 2 * (s + 1))
                                    if b == 0:
                                        pe.wait_ge(s_wlo, PIECES * (e + 1))
                                wait(pe, s_h32, k - 1)
                                n = 0
                                for kk in range(2):
                                    for w, x in ((w1_hi, xT_hi), (w1_hi, xT_lo), (w1_lo, xT_hi)):
                                        mm = pe.matmul(p_h[c % 2][:, 0:HALF], w[:, p, kk, c * 128:(c + 1) * 128],
                                                       x[:, b, kk, :], start=n == 0, stop=n == 5)
                                        n += 1
                                mm.then_inc(s_hmm, 1)
                            if c in (3, 4) and inside(s + 1, 2 * E):
                                pe.wait_ge(s_xn, BI * (s + 2))
                                wait(pe, s_xlo, 2 * (s + 1))
                                for i in range(BI):
                                    mm = pe.transpose(p_x[c - 3][:, i * SP_:(i + 1) * SP_],
                                                      xn[:, i, (c - 3) * 128:(c - 2) * 128], ident[0:SP_, 0:SP_])
                                mm.then_inc(s_tr, 1)
                            late = c < 2
                            if inside(s - 1, 2 * E) if late else inside(e, E):
                                cy, by = (c - 2) % FC, 1 - b if late else b
                                py = 1 - p if late and b == 0 else p
                                pe.wait_ge(s_hlo, k - 1)
                                if cy == 0:
                                    wait(pe, s_yb, 2 * (s - 1))
                                for i in range(BI):
                                    n = 0
                                    for a, w in ((h_hi, w2_hi), (h_hi, w2_lo), (h_lo, w2_hi)):
                                        mm = pe.matmul(p_o[by][i // 2][0:SP_, (i % 2) * D:(i % 2 + 1) * D],
                                                       a[:, cy % 4, i * SP_:(i + 1) * SP_], w[:, py, cy, :],
                                                       start=cy == 0 and n == 0 and i % 2 == 0,
                                                       stop=cy == FC - 1 and n == 2, skip_group_check=True)
                                        n += 1
                                mm.then_inc(s_ymm, 1)
                run(pe, -1, E + 1, step)

            @block.vector
            def _(dve):
                dve.wait_ge(e_b2, 16)
                dve.wait_ge(e_b1, 1)

                def step(e, p, div):
                    for b in range(2):
                        s = e * 2 + b
                        for c in range(FC):
                            k = e * 2 * FC + (b * FC + c)
                            if inside(e, E):
                                dve.wait_ge(s_hhi, k + 1)
                                wait(dve, s_ymm, k - 3)
                                dve.tensor_tensor(h_lo[:, c % 4, :], h32[:, c % 4, :], h_hi[:, c % 4, :].bitcast(F32),
                                                  ALU.subtract).then_inc(s_hlo, 1)
                            if c == 0 and inside(s + 1, 2 * E):
                                to = (2 * p + b + 1) % 4
                                dve.wait_ge(s_rows[to], 16 * (div(b, 2) + 1))
                                wait(dve, s_tr, 2 * (s + 1))
                                for i in range(BI):
                                    a = rows[:, to, i, :]
                                    dve.tensor_scalar(xn[:, i, :], a[:, 0:D], a[:, MEAN:MEAN + 1], a[:, RSTD:RSTD + 1],
                                                      ALU.subtract, ALU.mult).then_inc(s_xn, 1)
                                wait(dve, s_put[1 - b], 16 * BI * (e - 1 + b))
                                dve.tensor_copy(token[:, to, :], rows[:, to, :, TOKEN]).then_inc(s_tok, 1)
                            if c in (4, 5) and inside(s + 1, 2 * E):
                                dve.wait_ge(s_xhi, 2 * (s + 1) + c - 3)
                                dve.tensor_tensor(xT_lo[:, 1 - b, c - 4, :], p_x[c - 4][:, 0:HALF],
                                                  xT_hi[:, 1 - b, c - 4, :].bitcast(F32), ALU.subtract).then_inc(s_xlo, 1)
                            if b == 1 and inside(e + 1, E):
                                dve.wait_ge(s_whi, PIECES * (e + 1) + c + 1)
                                dve.tensor_tensor(piece(w1_lo, w2_lo, c, 1 - p), piece(w1_raw, w2_raw, c),
                                                  piece(w1_hi, w2_hi, c, 1 - p).bitcast(F32),
                                                  ALU.subtract).then_inc(s_wlo, 1)
                                if c == 7:
                                    wait(dve, s_h32, 2 * FC * e)
                                    dve.tensor_scalar(b1_now[:, 1 - p, :], b1_T[:, bass.ds(e * FC + FC, FC)], 1.0, None,
                                                      ALU.mult).then_inc(s_b1, 1)
                            if c == 1 and inside(s - 1, 2 * E):
                                dve.wait_ge(s_ymm, FC * s)
                                wait(dve, s_z, BI * (s - 1))
                                for i in range(2):
                                    dve.tensor_tensor(
                                        yb[:, i * 2 * D:(i + 1) * 2 * D].rearrange("p (i d) -> p i d", i=2),
                                        p_o[1 - b][i][0:SP_, :].rearrange("p (i d) -> p i d", i=2),
                                        b2_all[:, bass.ds(e + (b - 1), 1), :].to_broadcast([SP_, 2, D]),
                                        ALU.add).then_inc(s_yb, 1)
                            if c == 3 and inside(s - 1, 2 * E):
                                dve.wait_ge(s_z, BI * s)
                                dve.tensor_scalar(big[:], z[:], FLT_MAX, None, ALU.is_gt).then_inc(s_cmp, 1)
                                dve.tensor_scalar(fin[:], z[:], 0.0, 0.0, ALU.mult, ALU.is_equal).then_inc(s_cmp, 1)
                                dve.wait_ge(s_cmp, 2 * s)
                                wait(dve, s_res, s - 1)
                                dve.scalar_tensor_tensor(out=alt[:], in0=z[:], scalar=-FLT_MAX, in1=big[:], op0=ALU.is_lt,
                                                         op1=ALU.subtract).then_inc(s_alt, 1)
                            if c == 7 and inside(s - 1, 2 * E):
                                dve.wait_ge(s_alt2, s)
                                dve.sem_inc(e_met[1], 1)
                                dve.copy_predicated(alt[:], fin[:].bitcast(U32), z[:]).then_inc(s_sel, 1)
                                dve.wait_ge(s_sel, s)
                                wait(dve, s_put[1 - b], 16 * BI * (e - 1 + b))
                                dve.tensor_tensor(res[:, 1 - b, :, :], rows[:, (2 * p + b - 1) % 4, :, 0:D],
                                                  alt[:].rearrange("p (i d) -> p i d", i=BI), ALU.add).then_inc(s_res, 1)
                run(dve, -1, E + 1, step)


FIN_ACC = [2 * G + 8, 2 * G + 16]
FIN_X5 = 2 * G + 16 + G

_INS = ["x", "src", "dst", "wg", "attn_l", "attn_r", "wqkvT", "bqkv", "wprojT", "bproj", "temp", "gate_w", "gate_b",
        "w1", "b1", "w2", "b2", "consts"]


def kernel(**inp):
    import concourse.bacc as bacc
    from concourse.bass_utils import run_bass_kernel_spmd as launch

    c = np.ascontiguousarray
    arrays = {
        "x": c(inp["x"]), "src": c(inp["src"][:N]), "dst": c(inp["dst"][:N]),
        "wg": c(inp["L0_gnn_weight"]), "attn_l": c(inp["L0_gnn_attn_l"]).reshape(-1),
        "attn_r": c(inp["L0_gnn_attn_r"]).reshape(-1), "wqkvT": c(inp["L0_mix_Wqkv"].T),
        "bqkv": c(inp["L0_mix_bqkv"]), "wprojT": c(inp["L0_mix_Wproj"].T), "bproj": c(inp["L0_mix_bproj"]),
        "temp": c(inp["L0_mix_temperature"]).reshape(-1), "gate_w": c(inp["L0_ffn_gate_w"]),
        "gate_b": c(inp["L0_ffn_gate_b"]), "w1": c(inp["L0_ffn_w1"]), "b1": c(inp["L0_ffn_b1"]),
        "w2": c(inp["L0_ffn_w2"]), "b2": c(inp["L0_ffn_b2"]), "consts": constants(),
    }
    nc = bacc.Bacc("TRN2", target_bir_lowering=False, num_devices=1)
    args = [nc.dram_tensor("in_" + k, arrays[k].shape, mybir.dt.from_np(arrays[k].dtype), kind="ExternalInput").ap()
            for k in _INS]
    out = nc.dram_tensor("out", (N, D), F32, kind="ExternalOutput").ap()
    table = nc.dram_tensor("table", (N, TW), F32, kind="Internal").ap()
    alr_table = nc.dram_tensor("alr_table", (N, 2 * GH), F32, kind="Internal").ap()
    slots = nc.dram_tensor("slots", (E * SLOTS, RW), F32, kind="Internal").ap()
    build(nc, *args, out, table, alr_table, slots)
    r = launch(nc, [{"in_" + k: v for k, v in arrays.items()}], core_ids=[0])
    return r.results[0]["out"]
```

```python
from contextlib import ExitStack

import numpy as np

import concourse.bass as bass
from concourse import mybir

F32 = mybir.dt.float32
F32R = mybir.dt.float32r
BF16 = mybir.dt.bfloat16
I32 = mybir.dt.int32
U32 = mybir.dt.uint32
ALU = mybir.AluOpType
ACT = mybir.ActivationFunctionType
AX_X = mybir.AxisListType.X

N, D = 6250, 256
PT, TILES = 125, 50
PAIRS, NP = TILES // 2, 2 * PT
GH, GD = 4, 64
H, HD = 8, 32
G, R = 2, 4
ND = HD // 2
NF = ND * HD
CH = NF // 128
E, F = 8, 1024
CAP = -(-5 * N // (4 * E))
SP_, SI = 123, 8
SLOTS = SP_ * SI
HALF = SI // 2 * SP_
FC = F // 128
LN_EPS = 1e-5
EPS = 1e-12
SCALE = float(HD) ** 0.25
WC = 3 * D + D + 2 * GH
KVW = 1 + HD + HD + ND
GW = NF + ND + 1
TW = D + GH
FIN_ACC, FIN_X5 = [15, 16], 18
MEAN, VAR, RSTD, GATE, TOKEN, RW = D, D + 1, D + 2, D + 3, D + 4, D + 5
NO_TOKEN = 65536.0
LIN = 1 + 2 * HD

C_ID, C_BLK, C_TRI, C_M4, C_M8 = 0, 128, 256, 384, 388
C_REV, C_TOK = 404, 420
NC_ = 470


def constants():
    c = np.zeros((128, NC_), np.float32)
    p = np.arange(128)
    c[:, C_ID:C_ID + 128] = np.eye(128)
    c[:, C_BLK:C_BLK + 128] = (p[:, None] // HD) == (p[None] // HD)
    c[:, C_TRI:C_TRI + 128] = p[:, None] <= p[None]
    c[:, C_M4:C_M4 + R] = (p[:, None] // HD) == np.arange(R)
    for g in range(G):
        c[:, C_M8 + 8 * g:C_M8 + 8 * g + 8] = (p[:, None] // HD + R * g) == np.arange(H)
    c[:, C_REV:C_REV + E] = E - np.arange(E)
    c[0:PT, C_TOK:C_TOK + TILES] = np.arange(N).reshape(TILES, PT).T
    return c


def selections():
    s = np.zeros((128, 12 * 128), np.float32)
    for hp in range(2):
        for ch in range(CH):
            for f in range(128):
                d, i = divmod(ch * 128 + f, HD)
                for part in range(2):
                    for x in {i, (i + d) % HD}:
                        s[hp * 64 + part * HD + x, (hp * CH + ch) * 128 + f] = 1
    for b in range(H // 2):
        for hp in range(2):
            for i in range(ND):
                for part in range(2):
                    for x in (i, i + ND):
                        s[hp * 64 + part * HD + x, 2 * CH * 128 + b * 128 + (2 * b + hp) * ND + i] = 1
    return s


def wait(eng, sem, n):
    if not (isinstance(n, int) and n <= 0):
        eng.wait_ge(sem, n)


def inside(t, count):
    return not isinstance(t, int) or 0 <= t < count


def pipeline(eng, first, last, loop_from, loop_to, step, turn=2):
    def div(t):
        return lambda d, n: (t + d) // n

    for t in range(first, loop_from):
        step(t, t % turn, div(t))
    with eng.Fori(0, (loop_to - loop_from) // turn) as i:
        for u in range(turn):
            t = loop_from + u
            step(i * turn + t, t % turn, lambda d, n, t=t: i * (turn // n) + (t + d) // n)
    for t in range(loop_to, last):
        step(t, t % turn, div(t))


def view(ap, offset, dims):
    return bass.AP(tensor=ap.tensor, offset=ap.offset + offset, ap=[list(ap.ap[0])] + dims)


def build(nc, x, src, dst, wg, attn_l, attn_r, wqkvT, bqkv, wprojT, bproj, temp, gate_w, gate_b, w1, b1, w2, b2,
          consts, pair_sel, out, table, alr_table, slots):
    x_v = x.rearrange("(t p) d -> p t d", p=PT)
    out_v = out.rearrange("(t p) d -> p t d", p=PT)
    table_v = table.rearrange("(t p) d -> p t d", p=PT)
    alr_v = alr_table.rearrange("(t p) d -> p t d", p=PT)

    with ExitStack() as whole:
        def sem(name):
            return whole.enter_context(nc.semaphore(name))

        cst = whole.enter_context(nc.sbuf_tensor("cst", [128, NC_], F32))
        ident = cst[:, C_ID:C_ID + 128]
        q_full = whole.enter_context(nc.sbuf_tensor("q_all", [128, TILES, D], F32))
        q_all = q_full[0:PT]
        first = {n: sem("first_" + n) for n in ("w1", "w2", "b")}
        with ExitStack() as nodes:
            def keep(name, shape, dt=F32):
                return nodes.enter_context(nc.sbuf_tensor(name, shape, dt))

            x_all = keep("x_all", [PT, TILES, D])
            idx_all = keep("idx_all", [PT, 2, TILES], I32)
            coef = keep("coef", [128, G, CH, 128])
            coef5 = keep("coef5", [128, G, 128])
            lin = keep("lin", [128, G, 128])
            gram = keep("gram", [128, G, 128])
            sums = keep("sums", [128, 2 * 66 + 2 * 18])
            build_a(nc, sem, ExitStack(), x_v, src, dst, wg, attn_l, attn_r, wqkvT, bqkv, temp, consts, table_v,
                    alr_v, slots, x_all, q_all, idx_all, cst, ident, coef, coef5, lin, gram, sums)
            build_b(nc, sem, ExitStack(), wprojT, bproj, gate_w, gate_b, table, alr_table, out_v, slots, x_all,
                    q_full, pair_sel, idx_all, cst, ident, coef, coef5, lin, gram, sums,
                    lambda sp: load_first(sp, q_full, first, w1, b1, w2, b2))
        build_experts(nc, sem, ExitStack(), w1, w2, slots, out, ident, q_full, first)


def build_a(nc, sem, scope, x_v, src, dst, wg, attn_l, attn_r, wqkvT, bqkv, temp, consts, table_v, alr_v,
            slots, x_all, q_all, idx_all, cst, ident, coef, coef5, lin, gram, sums):
    with scope:
        def sb(name, shape, dt=F32):
            return scope.enter_context(nc.sbuf_tensor(name, shape, dt))

        def ps(name):
            return scope.enter_context(nc.psum_tensor(name, [128, 512], F32))

        w_raw = sb("w_raw", [128, 2, WC])
        w_hi = sb("w_hi", [128, 2, WC], F32R)
        w_lo = sb("w_lo", [128, 2, WC], F32R)
        b_raw = q_all[0:2, 40:43, :].rearrange("p t d -> p (t d)")
        b_hi = sb("b_hi", [2, 3 * D], F32R)
        b_lo = q_all[0:2, 43:46, :].rearrange("p t d -> p (t d)")
        b_two = sb("b_two", [2, 3 * D], F32R)
        ones2 = sb("ones2", [2, PT], F32R)
        floor2 = sb("floor2", [PT, 2 * H])
        gain = sb("gain", [PT, 2 * H])
        eps_t = sb("eps_t", [PT, 1])
        FILLS_A, BI_A = 24, 4
        BLANK = E * SLOTS // FILLS_A
        blank = sb("blank", [BLANK // BI_A, BI_A, RW])
        idx_raw = q_all[0:TILES, 46, 0:2 * PT].rearrange("t (n p) -> t n p", n=2).bitcast(I32)
        idx_f = q_all[0:TILES, 47, 0:2 * PT].rearrange("t (n p) -> t n p", n=2)
        stats = sb("stats", [PT, 2, 6])
        mv = sb("mv", [PT, 4, 2])
        std = sb("std", [PT, 2])
        rstd = sb("rstd", [PT, 2])
        xn = sb("xn", [PT, 2, D])
        xT_hi = sb("xT_hi", [128, 2, 2, PT], F32R)
        xT_lo = sb("xT_lo", [128, 2, 2, PT], F32R)
        qk_full = sb("qk", [128, 2, 2 * D])
        sq_full = sb("qk_sq", [128, 2, 2 * D])
        qk, qk_sq = qk_full[0:PT], sq_full[0:PT]
        attn, attn_w = qk_full[:, 0, :].rearrange("p (a n) -> p a n", a=2), sq_full[:, 0, :].rearrange("p (a n) -> p a n", a=2)
        ss = sb("ss", [PT, 2, 2 * H])
        ssm = sb("ssm", [PT, 2, 2 * H])
        norm = sb("norm", [PT, 2, 2 * H])
        rnorm = sb("rnorm", [PT, 2, 2 * H])
        fac = sb("fac", [PT, 2, 2 * H])
        kv = sb("kv", [PT, 2, H, KVW])
        feat_full = sb("feat", [128, 2, H, GW])
        feat = feat_full[0:PT]
        rest = feat_full[:].rearrange("p s h w -> p (s h w)")
        t_st = sb("t_st", [PT, 2, TW])
        alr = sb("alr", [PT, TILES, 2 * GH])
        acc_sb = rest[:, 0:G * NF].rearrange("p (g f) -> p g f", g=G)
        pad = rest[:, G * NF:G * NF + G * (ND - 1) * 2 * HD].rearrange("p (g d i) -> p g d i", g=G, d=ND - 1)
        dsum = sb("dsum", [128, G, 3, HD])
        x5 = sb("x5", [128, G, H, ND])

        p_t = [ps("p_t0"), ps("p_t1")]
        p_qk = [ps("p_qk0"), ps("p_qk1")]
        p_vx = ps("p_vx")
        p_acc = [ps("p_acc0"), ps("p_acc1")]
        p_sum = ps("p_sum")

        s_cst, s_w, s_bias = sem("s_cst"), sem("s_w"), sem("s_bias")
        s_init, s_zero = sem("s_init"), sem("s_zero")
        s_ild, s_if, s_it, s_idx_a = sem("s_ild"), sem("s_if"), sem("s_it"), sem("s_idx_a")
        s_prep, s_whi = sem("s_prep"), sem("s_whi")
        s_x = [sem("s_x0"), sem("s_x1")]
        s_stat, s_mv, s_std, s_rstd, s_xn = sem("s_stat"), sem("s_mv"), sem("s_std"), sem("s_rstd"), sem("s_xn")
        s_tp, s_hi, s_lo = sem("s_tp"), sem("s_hi"), sem("s_lo")
        s_alrmm, s_qkmm, s_vxmm = sem("s_alrmm"), sem("s_qkmm"), sem("s_vxmm")
        s_alr, s_ar, s_qk, s_v, s_xt = sem("s_alr"), sem("s_ar"), sem("s_qk"), sem("s_v"), sem("s_xt")
        s_sq, s_ss, s_ssm, s_norm, s_rn, s_fac = (sem("s_sq"), sem("s_ss"), sem("s_ssm"), sem("s_norm"),
                                                  sem("s_rn"), sem("s_fac"))
        s_kn, s_qn, s_wrap, s_d16, s_kk, s_kv = (sem("s_kn"), sem("s_qn"), sem("s_wrap"), sem("s_d16"),
                                                 sem("s_kk"), sem("s_kv"))
        s_tst = [sem("s_tst0"), sem("s_tst1")]
        s_bp = sem("s_bp")
        s_kkp, s_acc = sem("s_kkp"), sem("s_acc")
        s_met = [sem("s_met_dve"), sem("s_met_pool")]
        s_fin, s_ct = sem("s_fin"), sem("s_ct")
        W_READY = 6

        PH = 2

        def pairs(eng, u, g, r0, r1):
            k = kv[:, u, R * g + r0:R * g + r0 + 1, 1 + HD:2 + HD]
            return eng.tensor_tensor(
                feat[:, u, R * g + r0:R * g + r1, 0:NF].rearrange("p h (d i) -> p h d i", d=ND),
                view(k, 0, [[KVW, r1 - r0], [0, ND], [1, HD]]), view(k, 0, [[KVW, r1 - r0], [1, ND], [1, HD]]), ALU.mult)

        def run(eng, first, last, step):
            pipeline(eng, first, last, 4, 46, step)

        with nc.Block() as block:
            @block.sync
            def _(sp):
                sp.dma_start(x_all[:, 0, :], x_v[:, 0, :]).then_inc(s_x[0], 16)
                sp.dma_start(w_raw[:, :, 3 * D:4 * D], wg.rearrange("(k p) n -> p k n", p=128)).then_inc(s_w, 16)
                sp.dma_start(w_raw[:, :, 0:3 * D], wqkvT.rearrange("(k p) n -> p k n", p=128)).then_inc(s_w, 16)
                sp.dma_start(x_all[:, 1, :], x_v[:, 1, :]).then_inc(s_x[1], 16)
                sp.dma_start(b_raw, bqkv.partition_broadcast(2)).then_inc(s_bias, 16)
                sp.wait_ge(s_init, 3)
                sp.dma_start(gain[:, 0:H], temp.partition_broadcast(PT)).then_inc(s_bias, 16)

                for t in (2, 3):
                    sp.wait_ge(s_x[t % 2], 16)
                    sp.dma_start(x_all[:, t, :], x_v[:, t, :]).then_inc(s_x[t % 2], 16)

                def step(t, u, div):
                    if u == 0 and inside(t, 2 * FILLS_A):
                        sp.dma_start(slots[bass.ds(t * (BLANK // 2), BLANK), :].rearrange("(p i) d -> p i d", i=BI_A),
                                     blank[:]).then_inc(s_zero, 16)
                    if inside(t + 4, TILES):
                        sp.wait_ge(s_x[u], (div(0, 2) + 2) * 16)
                        sp.dma_start(x_all[:, t + 4, :], x_v[:, t + 4, :]).then_inc(s_x[u], 16)
                    if inside(t - 1, TILES):
                        sp.wait_ge(s_xt, t)
                        sp.wait_ge(s_ar, t)
                        sp.dma_start(table_v[:, t - 1, :], t_st[:, 1 - u, :]).then_inc(s_tst[1 - u], 16)
                run(sp, 0, TILES + 1, step)
                sp.wait_ge(s_alr, TILES)
                sp.dma_start(alr_v, alr[:]).then_inc(s_zero, 16)
                sp.wait_ge(s_zero, 16 * (FILLS_A + 1))
                sp.wait_ge(s_tst[0], 16 * TILES // 2)
                sp.wait_ge(s_tst[1], 16 * TILES // 2)

            @block.gpsimd
            def _(pool):
                pool.memset(blank[:, :, 0:TOKEN], 0.0).then_inc(s_init, 1)
                pool.memset(blank[:, :, TOKEN:RW], NO_TOKEN).then_inc(s_init, 1)
                pool.memset(gain[:], 1.0).then_inc(s_init, 1)
                pool.memset(eps_t[:], LN_EPS).then_inc(s_init, 1)
                pool.memset(floor2[:, 0:H], (EPS / SCALE) ** 2).then_inc(s_init, 1)
                pool.memset(floor2[:, H:2 * H], EPS ** 2).then_inc(s_init, 1)
                pool.memset(kv[:, :, :, 0:1], 1.0).then_inc(s_init, 1)
                pool.memset(feat[:, :, :, GW - 1:GW], 1.0).then_inc(s_init, 1)

                pool.wait_ge(s_bias, 32)
                pool.wait_ge(s_cst, 16)
                pool.tensor_scalar(b_hi[:], b_raw, 1.0, None, ALU.mult).then_inc(s_bp, 1)
                pool.wait_ge(s_bp, 1)
                pool.tensor_tensor(b_lo, b_raw, b_hi[:].bitcast(F32), ALU.subtract).then_inc(s_bp, 1)
                pool.wait_ge(s_bp, 2)
                pool.tensor_scalar(b_raw, b_hi[:].bitcast(F32), ident[0:2, 0:1], None, ALU.mult).then_inc(s_bp, 1)
                pool.tensor_scalar(b_lo, b_lo, ident[0:2, 1:2], None, ALU.mult).then_inc(s_bp, 1)
                pool.wait_ge(s_bp, 4)
                pool.tensor_tensor(b_two[:], b_lo, b_raw, ALU.add).then_inc(s_bp, 1)

                def step(t, u, div):
                    pool.wait_ge(s_fac, t + 1)
                    pool.wait_ge(s_qk, t + 1)
                    wait(pool, s_kv, t - 1)
                    wait(pool, s_kk, 2 * (t - 1))
                    k = kv[:, u, :, 1 + HD:1 + 2 * HD]
                    pool.tensor_tensor(k, qk[:, u, D:2 * D].rearrange("p (h d) -> p h d", h=H),
                                       fac[:, u, H:2 * H].unsqueeze(2).to_broadcast([PT, H, HD]),
                                       ALU.mult).then_inc(s_kn, 1)
                    pool.wait_ge(s_kn, t + 1)
                    pool.sem_inc(s_met[1], 1)
                    pool.tensor_scalar(kv[:, u, :, 1 + 2 * HD:KVW], kv[:, u, :, 1 + HD:1 + HD + ND], 1.0, None,
                                       ALU.mult).then_inc(s_wrap, 1)
                    pool.wait_ge(s_wrap, t + 1)
                    pairs(pool, u, 1, PH, R).then_inc(s_kkp, 1)
                    pool.tensor_tensor(feat[:, u, :, NF:NF + ND], kv[:, u, :, 1 + HD:1 + HD + ND],
                                       kv[:, u, :, 1 + HD + ND:1 + 2 * HD], ALU.mult).then_inc(s_d16, 1)
                    pool.tensor_tensor(q_all[:, t, :].rearrange("p (h d) -> p h d", h=H),
                                       qk[:, u, 0:D].rearrange("p (h d) -> p h d", h=H),
                                       fac[:, u, 0:H].unsqueeze(2).to_broadcast([PT, H, HD]),
                                       ALU.mult).then_inc(s_qn, 1)
                run(pool, 0, TILES, step)
                pool.wait_ge(s_qn, TILES)

            @block.scalar
            def _(act):
                for n, a in enumerate((attn_r, attn_l)):
                    act.dma_start(attn[:, n, :], a.partition_broadcast(128)).then_inc(s_w, 16)
                for n, a in enumerate((src, dst)):
                    act.dma_start(idx_raw[:, n, :], a.rearrange("(t p) -> t p", p=PT)).then_inc(s_ild, 16)
                act.dma_start(cst[:], consts).then_inc(s_cst, 16)
                act.wait_ge(s_w, 64)
                act.activation(w_hi[:, :, 0:4 * D], w_raw[:, :, 0:4 * D], ACT.Copy).then_inc(s_whi, 1)
                act.wait_ge(s_prep, 4)
                act.activation(w_hi[:, :, 4 * D:WC], w_raw[:, :, 4 * D:WC], ACT.Copy).then_inc(s_whi, 1)
                act.wait_ge(s_init, 8)

                def step(t, u, div):
                    if inside(t + 1, TILES):
                        act.wait_ge(s_tp, t + 2)
                        wait(act, s_vxmm, t)
                        wait(act, s_lo, t)
                        act.activation(xT_hi[:, 1 - u, :, :].rearrange("p k n -> p (k n)"),
                                       p_t[1 - u][:, 0:2 * PT], ACT.Copy).then_inc(s_hi, 1)
                    if inside(t, TILES):
                        act.wait_ge(s_alrmm, t + 1)
                        act.activation(alr[:, t, :], p_t[u][0:PT, 2 * PT:2 * PT + 2 * GH], ACT.Copy).then_inc(s_alr, 1)
                        wait(act, s_tst[u], div(0, 2) * 16)
                        act.activation(t_st[:, u, D:TW], p_t[u][0:PT, 2 * PT:2 * PT + GH], ACT.Copy).then_inc(s_ar, 1)
                        act.wait_ge(s_qkmm, t + 1)
                        wait(act, s_qn, t - 1)
                        act.activation(qk[:, u, :], p_qk[u][0:PT, :], ACT.Copy).then_inc(s_qk, 1)
                        act.wait_ge(s_qk, t + 1)
                        wait(act, s_ss, t - 1)
                        act.activation(qk_sq[:, u, :], qk[:, u, :], ACT.Square).then_inc(s_sq, 1)
                        act.wait_ge(s_ssm, t + 1)
                        wait(act, s_rn, t - 1)
                        act.activation(norm[:, u, :], ssm[:, u, :], ACT.Sqrt).then_inc(s_norm, 1)
                        act.wait_ge(s_vxmm, t + 1)
                        wait(act, s_kv, t - 1)
                        act.activation(kv[:, u, :, 1:1 + HD],
                                       p_vx[0:PT, 0:D].rearrange("p (h d) -> p h d", h=H), ACT.Copy).then_inc(s_v, 1)
                        act.activation(t_st[:, u, 0:D], p_vx[0:PT, D:2 * D], ACT.Copy).then_inc(s_xt, 1)
                    if inside(t + 3, TILES):
                        act.wait_ge(s_mv, t + 4)
                        wait(act, s_rstd, t + 2)
                        act.activation(std[:, 1 - u:2 - u], mv[:, 1 - u, 1:2], ACT.Sqrt,
                                       bias=eps_t[:, 0:1]).then_inc(s_std, 1)
                run(act, -3, TILES, step)
                act.wait_ge(s_kv, TILES)
                for g in range(G):
                    act.activation(acc_sb[:, g, :], p_acc[g][:, :], ACT.Copy).then_inc(s_acc, 1)
                for g in range(G):
                    act.wait_ge(s_acc, g + 1)
                    act.activation(pad[:, g, :, HD:2 * HD], acc_sb[:, g, HD:NF].rearrange("p (d i) -> p d i", i=HD),
                                   ACT.Copy).then_inc(s_acc, 1)

            @block.tensor
            def _(pe):
                pe.wait_ge(s_cst, 16)
                pe.wait_ge(s_init, 8)
                pe.wait_ge(s_if, 1)
                for n in range(2):
                    mm = pe.transpose(p_acc[0][0:PT, n * TILES:(n + 1) * TILES], idx_f[:, n, :], ident[0:TILES, 0:TILES])
                mm.then_inc(s_it, 1)
                pe.wait_ge(s_idx_a, 1)

                def project(bank, u, c0, bias, done, with_alr=None):
                    passes = [(xT, w, k) for k in range(2) for xT, w in ((xT_hi, w_hi), (xT_hi, w_lo), (xT_lo, w_hi))]
                    for i, (xT, w, k) in enumerate(passes):
                        last = i == len(passes) - 1
                        mm = pe.matmul(bank[0:PT, :], xT[:, u, k, :], w[:, k, c0:c0 + 2 * D], start=i == 0, stop=last)
                        if i == 0:
                            pe.matmul(bank[0:PT, 0:bias], ones2[:], b_two[:, c0:c0 + bias], start=False, stop=False)
                        if last:
                            mm.then_inc(done, 1)
                        if with_alr:
                            mm = pe.matmul(p_t[u][0:PT, 2 * PT:2 * PT + 2 * GH], xT[:, u, k, :], w[:, k, 4 * D:WC],
                                           start=i == 0, stop=last)
                            if last:
                                mm.then_inc(with_alr, 1)

                def step(t, u, div):
                    if inside(t, TILES):
                        pe.wait_ge(s_hi, t + 1)
                        pe.wait_ge(s_lo, t + 1)
                    if inside(t + 1, TILES):
                        pe.wait_ge(s_xn, t + 2)
                        wait(pe, s_alr, t)
                        wait(pe, s_ar, t)
                        for k in range(2):
                            mm = pe.transpose(p_t[1 - u][:, k * PT:(k + 1) * PT], xn[:, 1 - u, k * 128:(k + 1) * 128],
                                              ident[0:PT, 0:PT])
                        mm.then_inc(s_tp, 1)
                    if inside(t, TILES):
                        wait(pe, s_qk, t - 1)
                        if isinstance(t, int) and t == 0:
                            pe.wait_ge(s_whi, 2)
                            pe.wait_ge(s_prep, W_READY)
                            pe.wait_ge(s_bp, 5)
                        project(p_qk[u], u, 0, 2 * D, s_qkmm, s_alrmm)
                    if inside(t - 2, TILES):
                        pe.wait_ge(s_kk, 2 * (t - 1))
                        pe.wait_ge(s_kkp, t - 1)
                        pe.wait_ge(s_d16, t - 1)
                        pe.wait_ge(s_v, t - 1)
                        first = isinstance(t, int) and t == 2
                        last = isinstance(t, int) and t == TILES + 1
                        for g in range(G):
                            for r in range(R):
                                q = slice(HD * r, HD * r + HD)
                                pe.matmul(p_acc[g][q, :], kv[:, u, R * g + r, 1:1 + HD], feat[:, u, R * g + r, 0:NF],
                                          start=first, stop=last, skip_group_check=True)
                            for r in range(R):
                                q = slice(HD * r, HD * r + HD)
                                pe.matmul(p_sum[q, 66 * g:66 * g + LIN], kv[:, u, R * g + r, 1 + HD:1 + 2 * HD],
                                          kv[:, u, R * g + r, 0:LIN], start=first and g == 0, stop=last,
                                          skip_group_check=True)
                            for r in range(R):
                                q = slice(HD * r, HD * r + HD)
                                mm = pe.matmul(p_sum[q, 132 + 18 * g:132 + 18 * g + ND + 1],
                                               kv[:, u, R * g + r, 1:1 + HD], feat[:, u, R * g + r, NF:GW],
                                               start=False, stop=last, skip_group_check=True)
                        mm.then_inc(s_kv, 1)
                    if inside(t, TILES):
                        wait(pe, s_v, t)
                        wait(pe, s_xt, t)
                        project(p_vx, u, 2 * D, D, s_vxmm)
                run(pe, -1, TILES + 2, step)
                pe.wait_ge(s_xt, TILES)
                for g in range(G):
                    for c in range(CH):
                        if c == 0:
                            pe.wait_ge(s_fin, FIN_ACC[g])
                        mm = pe.transpose(p_t[g][:, c * 128:(c + 1) * 128], acc_sb[:, g, c * 128:(c + 1) * 128], ident)
                    mm.then_inc(s_ct, 1)
                pe.wait_ge(s_fin, FIN_X5)
                for g in range(G):
                    mm = pe.transpose(p_vx[:, g * 128:(g + 1) * 128], x5[:, g, :, :].rearrange("p h i -> p (h i)"),
                                      ident)
                mm.then_inc(s_ct, 1)

            @block.vector
            def _(dve):
                n = [0]

                def link(ins, done):
                    n[0] += 1
                    ins.then_inc(done, 1)
                    dve.wait_ge(done, n[0])

                dve.wait_ge(s_ild, 32)
                dve.tensor_copy(idx_f, idx_raw).then_inc(s_if, 1)
                dve.wait_ge(s_it, 1)
                dve.tensor_copy(idx_all[:].rearrange("p n t -> p (n t)"), p_acc[0][0:PT, 0:2 * TILES]).then_inc(s_idx_a, 1)
                dve.wait_ge(s_w, 64)
                for a in range(2):
                    aw = attn[:, a, :].unsqueeze(1).to_broadcast([128, 2, D])
                    link(dve.tensor_tensor(attn_w, w_raw[:, :, 3 * D:4 * D], aw, ALU.mult), s_prep)
                    link(dve.tensor_reduce(w_raw[:, :, 4 * D + GH * a:4 * D + GH * a + GH],
                                           attn_w.rearrange("p k (h d) -> p k h d", h=GH), AX_X, ALU.add), s_prep)
                dve.wait_ge(s_cst, 16)
                dve.tensor_copy(ones2[:], cst[0:2, C_BLK:C_BLK + 1].to_broadcast([2, PT])).then_inc(s_prep, 1)
                def step(t, u, div):
                    if inside(t + 2, TILES):
                        dve.wait_ge(s_std, t + 3)
                        wait(dve, s_xn, t + 1)
                        dve.reciprocal(rstd[:, u:u + 1], std[:, u:u + 1]).then_inc(s_rstd, 1)
                    if inside(t + 1, TILES):
                        dve.wait_ge(s_hi, t + 2)
                        wait(dve, s_vxmm, t)
                        dve.tensor_tensor(xT_lo[:, 1 - u, :, :].rearrange("p k n -> p (k n)"), p_t[1 - u][:, 0:2 * PT],
                                          xT_hi[:, 1 - u, :, :].rearrange("p k n -> p (k n)").bitcast(F32),
                                          ALU.subtract).then_inc(s_lo, 1)
                    if inside(t - 1, TILES):
                        dve.wait_ge(s_wrap, t)
                        wait(dve, s_kv, t - 2)
                        pairs(dve, 1 - u, 0, 0, R).then_inc(s_kk, 1)
                    if inside(t, TILES):
                        dve.wait_ge(s_sq, t + 1)
                        dve.tensor_reduce(ss[:, u, :], qk_sq[:, u, :].rearrange("p (h d) -> p h d", d=HD), AX_X,
                                          ALU.add).then_inc(s_ss, 1)
                    if inside(t + 3, TILES):
                        dve.wait_ge(s_x[1 - u], 16 * (div(0, 2) + 2 + u))
                        dve.bn_stats(stats[:, 1 - u, :], x_all[:, t + 3, :]).then_inc(s_stat, 1)
                    if inside(t, TILES):
                        dve.wait_ge(s_ss, t + 1)
                        wait(dve, s_norm, t - 1)
                        dve.tensor_tensor(ssm[:, u, :], ss[:, u, :], floor2[:], ALU.max).then_inc(s_ssm, 1)
                    if inside(t + 2, TILES):
                        dve.wait_ge(s_rstd, t + 3)
                        wait(dve, s_tp, t + 1)
                        dve.tensor_scalar(xn[:, u, :], x_all[:, t + 2, :], mv[:, u, 0:1], rstd[:, u:u + 1],
                                          ALU.subtract, ALU.mult).then_inc(s_xn, 1)
                    if inside(t + 3, TILES):
                        dve.wait_ge(s_stat, t + 4)
                        wait(dve, s_std, t + 2)
                        wait(dve, s_xn, t + 2)
                        dve.sem_inc(s_met[0], 1)
                        dve.bn_aggr(mv[:, 1 - u, :], stats[:, 1 - u, :]).then_inc(s_mv, 1)
                    if inside(t, TILES):
                        dve.wait_ge(s_norm, t + 1)
                        wait(dve, s_fac, t - 1)
                        dve.reciprocal(rnorm[:, u, :], norm[:, u, :]).then_inc(s_rn, 1)
                    if inside(t, TILES):
                        dve.wait_ge(s_rn, t + 1)
                        wait(dve, s_qn, t - 1)
                        wait(dve, s_kn, t - 1)
                        dve.tensor_tensor(fac[:, u, :], rnorm[:, u, :], gain[:], ALU.mult).then_inc(s_fac, 1)
                    if inside(t - 1, TILES):
                        pairs(dve, 1 - u, 1, 0, PH).then_inc(s_kk, 1)
                step(-3, 1, lambda d, n: (d - 3) // n)
                dve.wait_ge(s_whi, 2)
                dve.tensor_tensor(w_lo[:], w_raw[:], w_hi[:].bitcast(F32), ALU.subtract).then_inc(s_prep, 1)
                dve.wait_ge(s_bias, 32)
                dve.wait_ge(s_init, 8)
                run(dve, -2, TILES + 1, step)

                dve.wait_ge(s_kv, TILES)
                for g in range(G):
                    for c in (slice(66 * g, 66 * g + LIN), slice(132 + 18 * g, 132 + 18 * g + ND + 1)):
                        dve.tensor_copy(sums[:, c], p_sum[:, c]).then_inc(s_fin, 1)
                for g in range(G):
                    dve.wait_ge(s_acc, g + 1)
                    dve.tensor_copy(pad[:, g, :, 0:HD], acc_sb[:, g, HD:NF].rearrange("p (d i) -> p d i", i=HD)
                                    ).then_inc(s_fin, 1)
                for g in range(G):
                    dve.tensor_reduce(dsum[:, g, 0, :], view(acc_sb[:, g, HD:HD + 1], 0, [[1, HD], [HD, ND - 1]]),
                                      AX_X, ALU.add).then_inc(s_fin, 1)
                dve.wait_ge(s_fin, 8)
                for g in range(G):
                    dve.wait_ge(s_acc, G + g + 1)
                    dve.tensor_reduce(dsum[:, g, 1, :], view(pad[:, g, 0, HD - 1:HD], 0, [[1, HD], [2 * HD - 1, ND - 1]]),
                                      AX_X, ALU.add).then_inc(s_fin, 1)
                for g in range(G):
                    dve.wait_ge(s_fin, 9 + g)
                    dve.tensor_tensor(dsum[:, g, 2, :], dsum[:, g, 0, :], dsum[:, g, 1, :], ALU.add).then_inc(s_fin, 1)
                for g in range(G):
                    x16 = sums[:, 132 + 18 * g:132 + 18 * g + ND]
                    dve.wait_ge(s_fin, 11 + g)
                    dve.tensor_tensor(dsum[:, g, 0, :].rearrange("p (a i) -> p a i", a=2),
                                      dsum[:, g, 2, :].rearrange("p (a i) -> p a i", a=2),
                                      x16.unsqueeze(1).to_broadcast([128, 2, ND]), ALU.add).then_inc(s_fin, 1)
                for g in range(G):
                    dve.wait_ge(s_fin, 13 + g)
                    dve.tensor_tensor(acc_sb[:, g, 0:HD], acc_sb[:, g, 0:HD], dsum[:, g, 0, :], ALU.subtract
                                      ).then_inc(s_fin, 1)
                for g in range(G):
                    x16 = sums[:, 132 + 18 * g:132 + 18 * g + ND]
                    m8 = cst[:, C_M8 + 8 * g:C_M8 + 8 * g + 8]
                    dve.tensor_tensor(x5[:, g, :, :], x16.unsqueeze(1).to_broadcast([128, H, ND]),
                                      m8.unsqueeze(2).to_broadcast([128, H, ND]), ALU.mult).then_inc(s_fin, 1)
                for g in range(G):
                    m4 = cst[:, C_M4:C_M4 + R].unsqueeze(2).to_broadcast([128, R, HD])
                    for to, at, half in ((lin, 1, 1.0), (gram, 1 + HD, 0.5)):
                        s = sums[:, 66 * g + at:66 * g + at + HD].unsqueeze(1).to_broadcast([128, R, HD])
                        o = to[:, g, :].rearrange("p (r d) -> p r d", r=R)
                        dve.scalar_tensor_tensor(out=o, in0=s, scalar=half, in1=m4, op0=ALU.mult,
                                                 op1=ALU.mult).then_inc(s_fin, 1)
                for g in range(G):
                    dve.wait_ge(s_ct, g + 1)
                    dve.tensor_scalar(coef[:, g, :, :].rearrange("p c m -> p (c m)"), p_t[g][:, :], 0.5, None,
                                      ALU.mult).then_inc(s_fin, 1)
                dve.wait_ge(s_ct, G + 1)
                dve.tensor_scalar(coef5[:].rearrange("p g m -> p (g m)"), p_vx[:, 0:G * 128], 0.5, None,
                                  ALU.mult).then_inc(s_fin, 1)
                dve.wait_ge(s_fin, FIN_X5 + 2 * G + G + 1)


def build_b(nc, sem, scope, wprojT, bproj, gate_w, gate_b, table, alr_table, out_v, slots, x_all, q_full, pair_sel, idx_all,
            cst, ident, coef, coef5, lin, gram, sums, load_first):
    with scope:
        def sb(name, shape, dt=F32):
            return scope.enter_context(nc.sbuf_tensor(name, shape, dt))

        def ps(name):
            return scope.enter_context(nc.psum_tensor(name, [128, 512], F32))

        sel = sb("sel", [128, 12, 128], F32R)
        wproj = sb("wproj", [128, G, D])
        bproj_t = sb("bproj_t", [PT, D])
        gate_t = sb("gate_t", [128, 2, E])
        gateb_t = sb("gateb_t", [PT, E])
        ones_b, tri_b = sb("ones_b", [PT, PT], BF16), sb("tri_b", [PT, PT], BF16)
        row = sb("row", [PT, 4, 2, RW])
        lg = sb("lg", [PT, 2, 4, E])
        lgb, rd, rex, rw = (sb(n, [PT, 2, E]) for n in ("lgb", "rd", "rex", "rw"))
        pm = sb("pm", [PT, 2, E])
        rmax, rsum = sb("rmax", [PT, 2]), sb("rsum", [PT, 2])
        rev_max = sb("rev_max", [PT, 2, 2])
        one_hot = sb("one_hot", [PT, 2, 2, E], BF16)
        before = sb("before", [PT, 2, 2, E], BF16)
        pos, over, at = sb("pos", [PT, 2]), sb("over", [PT, 2]), sb("at", [PT, 2])
        slot = sb("slot", [PT, 2, 2], I32)
        eps2 = sb("eps2", [PT, 2])
        half2 = sb("half2", [PT, 2])
        q_st = sb("q_st", [PT, 2, 2 * D])
        q_hl = sb("q_hl", [PT, 2, 2 * H, 2, HD], F32R)
        q_hlT = sb("q_hlT", [128, 2, H // 2, NP], F32R)
        q_fT = sb("q_fT", [128, 2, G, NP])
        sq = sb("sq", [128, G, R, CH, NP])
        sq5 = sb("sq5", [128, 2, NP])
        w_t = sb("w_t", [128, G, NP])
        w_hi, w_lo = sb("w_hi_b", [128, G, NP], F32R), sb("w_lo_b", [128, G, NP], F32R)
        blk_r = sb("blk_r", [128, 128], F32R)
        y_t = sb("y_t", [128, G, NP])
        idx = sb("idx", [PT, 2, 2, 2], I32)
        rows = sb("rows", [PT, 2, 2, TW])
        alr_g = sb("alr_g", [PT, 2, 2, 2 * GH])
        ga, gl, gs, ge, gp = (sb(n, [PT, 2, GH]) for n in ("ga", "gl", "gs", "ge", "gp"))
        gmax, gsum, grec = sb("gmax", [PT, 2]), sb("gsum", [PT, 2]), sb("grec", [PT, 2])
        prod = sb("prod", [PT, 2, GH, GD])
        tmp = sb("tmp", [PT, 2, 2, GD])
        st2 = sb("st2", [PT, 2, 6])
        ve2 = sb("ve2", [PT, 2, 2])
        sel_raw = sq[:].rearrange("p g r c n -> p (g r c n)")[:, 0:12 * 128]
        q_all = q_full[0:PT]
        x_st = q_all[:, 0:4, :].rearrange("p (s u) d -> p s u d", s=2)
        x_T = q_full[:, 4:6, :].rearrange("p t d -> p (t d)")[:, 0:2 * NP].rearrange("p (k n) -> p k n", k=2)

        p_sel = [ps(f"p_sel{i}") for i in range(3)]
        p_y = [ps("p_y0"), ps("p_y1")]
        p_gram, p_tr, p_proj = ps("p_gram"), ps("p_tr"), ps("p_proj")

        b_ld, b_ini, b_src, b_sel = sem("b_ld"), sem("b_ini"), sem("b_src"), sem("b_sel")
        b_met = [sem("b_met_pool"), sem("b_met_dve")]
        s_qst, s_qhi, s_qlo = sem("s_qst"), sem("s_qhi"), sem("s_qlo")
        s_trh, s_trf, s_trx = sem("s_trh"), sem("s_trf"), sem("s_trx")
        s_evh, s_evf, s_evx = sem("s_evh"), sem("s_evf"), sem("s_evx")
        s_fill, s_sqd = sem("s_fill"), sem("s_sqd")
        s_gram, s_w2 = sem("s_gram"), sem("s_w2")
        s_yn = [sem("s_yn0"), sem("s_yn1")]
        s_den, s_rden, s_y = ([sem(f"{n}{g}") for g in range(G)] for n in ("s_den", "s_rden", "s_y"))
        s_proj, s_x2, s_st2, s_mv2, s_ve2, s_rs2 = (sem(n) for n in ("s_proj", "s_x2", "s_st2", "s_mv2", "s_ve2",
                                                                     "s_rs2"))
        s_xst, s_gate, s_gev = sem("s_xst"), sem("s_gate"), sem("s_gev")
        s_wh, s_wl = sem("s_wh"), sem("s_wl")
        s_route, s_rd, s_rex, s_oh, s_gt = sem("s_route"), sem("s_rd"), sem("s_rex"), sem("s_oh"), sem("s_gt")
        s_lgb, s_rmax, s_rw, s_rev, s_hot, s_rsum = (sem(n) for n in ("s_lgb", "s_rmax", "s_rw", "s_rev", "s_hot",
                                                                      "s_rsum"))
        s_pos, s_slot = sem("s_pos"), sem("s_slot")
        s_scat, s_out = ([sem(f"{n}{i}") for i in range(4)] for n in ("s_scat", "s_out"))
        s_idx, s_g = sem("s_idx"), [sem("s_g0"), sem("s_g1")]
        s_ga, s_gl, s_gmax, s_gs, s_ge, s_gsum, s_grec, s_gp, s_prod, s_tmp = (
            sem(n) for n in ("s_ga", "s_gl", "s_gmax", "s_gs", "s_ge", "s_gsum", "s_grec", "s_gp", "s_prod", "s_tmp"))
        s_xb, s_gadd = sem("s_xb"), sem("s_gadd")
        FILLS = 17
        LOADS = 4 * 16
        SEL_H = 6 * 128

        def run(eng, first, last, step):
            pipeline(eng, first, last, 7, 23, step, turn=4)

        def gate_and_positions(j):
            return 0 if inside(j - 3, TILES // 2) else 2, 4 if inside(j - 4, TILES // 2) else 2

        with nc.Block() as block:
            @block.sync
            def _(sp):
                sp.dma_start(sel_raw[:, 0:SEL_H], pair_sel[:, 0:SEL_H]).then_inc(b_src, 16)
                sp.dma_start(wproj[:], wprojT.rearrange("(g p) n -> p g n", p=128)).then_inc(b_ld, 16)
                sp.dma_start(bproj_t[:], bproj.partition_broadcast(PT)).then_inc(b_ld, 16)
                sp.dma_start(gate_t[:], gate_w.rearrange("(k p) n -> p k n", p=128)).then_inc(b_ld, 16)
                sp.dma_start(gateb_t[:], gate_b.partition_broadcast(PT)).then_inc(b_ld, 16)

                def step(j, r, div):
                    if isinstance(j, int) and j == TILES // 2 - 2:
                        sp.wait_ge(s_qst, TILES // 2)
                        load_first(sp)
                    sp.wait_ge(s_x2, j)
                    sp.dma_start(out_v[:, bass.ds(j * 2 - 2, 2), :], row[:, (r - 1) % 4, :, 0:D]
                                 ).then_inc(s_out[(r - 1) % 4], 16)
                run(sp, 1, TILES // 2 + 1, step)
                for i in range(4):
                    sp.wait_ge(s_out[i], 16 * len(range(i, TILES // 2, 4)))

            @block.gpsimd
            def _(pool):
                pool.memset(eps2[:], LN_EPS).then_inc(b_ini, 1)
                pool.memset(half2[:], -0.5).then_inc(b_ini, 1)
                pool.memset(ones_b[:], 1.0).then_inc(b_ini, 1)
                pool.memset(one_hot[:], 0.0).then_inc(b_ini, 1)
                pool.memset(before[:], 0.0).then_inc(b_ini, 1)
                pool.tensor_copy(tri_b[:], cst[0:PT, C_TRI:C_TRI + PT]).then_inc(b_ini, 1)
                pool.tensor_scalar(blk_r[:], cst[:, C_BLK:C_BLK + 128], 1.0, None, ALU.mult).then_inc(b_ini, 1)
                pool.wait_ge(b_ini, 7)

                def step(j, r, div):
                    p = r % 2
                    if inside(j, TILES // 2):
                        if isinstance(j, int) and j == 0:
                            pool.wait_ge(b_ld, LOADS)
                        xj = x_all[:, bass.ds(j * 2, 2), :]
                        pool.tensor_tensor(xj, xj, bproj_t[:].unsqueeze(1).to_broadcast([PT, 2, D]),
                                           ALU.add).then_inc(s_xb, 1)
                    if inside(j - 5, TILES // 2):
                        pool.wait_ge(s_slot, j - 4)
                        pool.wait_ge(s_gt, j - 4)
                        pool.sem_inc(b_met[0], 1)
                        for u in range(2):
                            pool.indirect_dma_start(
                                slots, bass.IndirectOffsetOnAxis(ap=slot[:, 1 - p, u:u + 1], axis=0),
                                row[:, (r - 5) % 4, u, :], None, bounds_check=E * SLOTS - 1,
                                oob_is_err=False).then_inc(s_scat[(r - 5) % 4], 16)
                    if inside(j, TILES // 2):
                        pool.wait_ge(s_gp, j + 1)
                        wait(pool, s_tmp, j)
                        pool.tensor_tensor(prod[:], rows[:, p, :, 0:D].rearrange("p t (h d) -> p t h d", h=GH),
                                           gp[:].unsqueeze(3).to_broadcast([PT, 2, GH, GD]), ALU.mult).then_inc(s_prod, 1)
                        pool.wait_ge(s_wh, j + 1)
                        wait(pool, s_yn[1], j)
                        pool.tensor_tensor(w_lo[:], w_t[:], w_hi[:].bitcast(F32), ALU.subtract).then_inc(s_wl, 1)
                    if inside(j - 1, TILES // 2):
                        pool.wait_ge(s_mv2, 2 * j)
                        pool.tensor_tensor(ve2[:, 1 - p, :], row[:, (r - 1) % 4, :, VAR], eps2[:],
                                           ALU.add).then_inc(s_ve2, 1)
                        pool.wait_ge(s_ve2, j)
                        pool.tensor_tensor(row[:, (r - 1) % 4, :, RSTD], ve2[:, 1 - p, :], half2[:],
                                           ALU.pow).then_inc(s_rs2, 1)
                    s = j + 2
                    if inside(s, TILES // 2):
                        wait(pool, s_g[p], 64 * (div(0, 2) + 1))
                        wait(pool, s_tmp, j + 1)
                        pool.sem_inc(b_met[0], 1)
                        pool.tensor_copy(idx[:, p, :, :], idx_all[:, :, bass.ds(j * 2 + 4, 2)]).then_inc(s_idx, 1)
                        pool.wait_ge(s_idx, j + 3)
                        pool.sem_inc(b_met[0], 1)
                        for u in range(2):
                            pool.indirect_dma_start(
                                rows[:, p, u, :], None, table,
                                bass.IndirectOffsetOnAxis(ap=idx[:, p, 1, u:u + 1], axis=0)).then_inc(s_g[p], 16)
                            pool.indirect_dma_start(
                                alr_g[:, p, u, :], None, alr_table,
                                bass.IndirectOffsetOnAxis(ap=idx[:, p, 0, u:u + 1], axis=0)).then_inc(s_g[p], 16)
                    if inside(j, TILES // 2):
                        pool.wait_ge(s_xb, j + 1)
                        pool.wait_ge(s_tmp, j + 1)
                        pool.sem_inc(b_met[0], 1)
                        x4 = xj.rearrange("p t (r d) -> p t r d", r=GH)
                        pool.tensor_tensor(x4, x4, tmp[:, p, :, :].unsqueeze(2).to_broadcast([PT, 2, GH, GD]),
                                           ALU.add).then_inc(s_gadd, 1)
                run(pool, -2, TILES // 2 + 5, step)
                for i in range(4):
                    pool.wait_ge(s_scat[i], 32 * len(range(i, TILES // 2, 4)))

            @block.scalar
            def _(act):

                act.dma_start(sel_raw[:, SEL_H:2 * SEL_H], pair_sel[:, SEL_H:2 * SEL_H]).then_inc(b_src, 16)

                def square(j, p, k):
                    act.wait_ge(s_fill, j * FILLS + k + 1)
                    if k == 8:
                        o, n = sq5[:, p, :], NP
                    else:
                        g, f = k // 9, k % 9
                        o = sq[:, g, f % 4, 2 * (f // 4):2 * (f // 4) + 2, :].rearrange("p c n -> p (c n)")
                        n = 2 * NP
                    act.activation(o, p_sel[k % 3][:, 0:n], ACT.Square).then_inc(s_sqd, 1)

                def step(j, r, div):
                    p = r % 2
                    main, nxt = inside(j, TILES // 2), inside(j + 1, TILES // 2)
                    for k in range(FILLS):
                        if main and k == 0 and isinstance(j, int) and j == 0:
                            act.wait_ge(b_sel, 1)
                        if main:
                            square(j, p, k)
                        if k == 6 and isinstance(j, int) and j == -1:
                            act.wait_ge(b_src, 32)
                            act.activation(sel[:].rearrange("p s m -> p (s m)"), sel_raw, ACT.Copy).then_inc(b_sel, 1)
                        if k == 2 and inside(j + 2, TILES // 2):
                            act.wait_ge(s_qst, j + 3)
                            wait(act, s_trh, 2 * (j + 1))
                            wait(act, s_qlo, j + 1)
                            act.activation(q_hl[:, p, :, 0, :], q_st[:, p, :].rearrange("p (h d) -> p h d", d=HD),
                                           ACT.Copy).then_inc(s_qhi, 1)
                        if nxt and k in (5, 8):
                            b = 2 * (k // 8)
                            act.wait_ge(s_trh, 2 * (j + 1) + k // 8 + 1)
                            act.activation(q_hlT[:, 1 - p, b:b + 2, :].rearrange("p b n -> p (b n)"),
                                           p_tr[:, 0:2 * NP], ACT.Copy).then_inc(s_evh, 1)
                        if main and k == 5:
                            act.wait_ge(s_gs, j + 1)
                            wait(act, s_gp, j)
                            act.activation(ge[:], gs[:], ACT.Exp).then_inc(s_ge, 1)
                        if main and k == 9:
                            act.wait_ge(s_w2, 2 * (j + 1))
                            wait(act, s_wl, j)
                            wait(act, s_yn[1], j)
                            act.activation(w_hi[:], w_t[:], ACT.Copy).then_inc(s_wh, 1)
                        if k == 9 and inside(j - 4, TILES // 2):
                            act.wait_ge(s_rd, j - 3)
                            wait(act, s_gt, j - 4)
                            act.activation(rex[:], rd[:], ACT.Exp).then_inc(s_rex, 1)
                        if nxt and k == 12:
                            act.wait_ge(s_trf, j + 2)
                            wait(act, s_w2, 2 * j)
                            act.activation(q_fT[:, 1 - p, :, :].rearrange("p g n -> p (g n)"), p_tr[:, 0:2 * NP],
                                           ACT.Copy).then_inc(s_evf, 1)
                        a, b = gate_and_positions(j)
                        if k == 16 and a < b:
                            act.wait_ge(s_gate, j - 2)
                            wait(act, s_lgb, j - 4)
                            act.activation(lg[:, p, a:b, :].rearrange("p t e -> p (t e)"), p_tr[0:PT, a * E:b * E],
                                           ACT.Copy).then_inc(s_gev, 1)
                        if k == 1 and inside(j - 3, TILES // 2):
                            act.wait_ge(s_trx, j - 2)
                            act.activation(x_T.rearrange("p k n -> p (k n)"), p_tr[:, 0:2 * NP],
                                           ACT.Copy).then_inc(s_evx, 1)
                run(act, -2, TILES // 2 + 4, step)

            @block.tensor
            def _(pe):

                def fill(j, p, k):
                    if k == 0:
                        if isinstance(j, int) and j == 0:
                            pe.wait_ge(b_sel, 1)
                            pe.wait_ge(b_ini, 7)
                            pe.wait_ge(b_ld, LOADS)
                        pe.wait_ge(s_evh, 2 * (j + 1))
                    if k >= 3:
                        pe.wait_ge(s_sqd, j * FILLS + k - 2)
                    else:
                        wait(pe, s_sqd, (j - 1) * FILLS + (16, 17, 15)[k])
                    bank = p_sel[k % 3]
                    if k == 8:
                        for b in range(H // 2):
                            mm = pe.matmul(bank[:, 0:NP], sel[:, 8 + b, :], q_hlT[:, p, b, :], start=b == 0,
                                           stop=b == H // 2 - 1)
                    else:
                        g, f = k // 9, k % 9
                        head = R * g + f % 4
                        for c in range(2):
                            ch = 2 * (f // 4) + c
                            mm = pe.matmul(bank[:, c * NP:(c + 1) * NP], sel[:, (head % 2) * CH + ch, :],
                                           q_hlT[:, p, head // 2, :], start=True, stop=True)
                    mm.then_inc(s_fill, 1)

                def contract(g, j, c):
                    pe.wait_ge(s_sqd, j * FILLS + 9 * g + 4 * (c // 2) + 4)
                    if c == 0:
                        wait(pe, s_y[g], j)
                    for r in range(R):
                        q = slice(HD * r, HD * r + HD)
                        pe.matmul(p_y[g][q, 0:NP], coef[:, g, c, q], sq[:, g, r, c, :], start=c == 0,
                                  stop=False, skip_group_check=True)

                def finish(g, j, p):
                    pe.wait_ge(s_sqd, j * FILLS + 9)
                    pe.matmul(p_y[g][:, 0:NP], coef5[:, g, :], sq5[:, p, :], start=False, stop=False,
                              skip_group_check=True)
                    pe.matmul(p_y[g][:, 0:NP], lin[:, g, :], q_fT[:, p, g, :], start=False, stop=True,
                              skip_group_check=True)

                def spread_norm(g, j, p):
                    pe.wait_ge(s_wl, j + 1)
                    for i, w in enumerate((w_hi, w_lo)):
                        mm = pe.matmul(p_y[g][:, NP:2 * NP], blk_r[:], w[:, g, :], start=i == 0, stop=i == 1,
                                       skip_group_check=True)
                    mm.then_inc(s_yn[g], 1)

                def turn_hl(j, p, i):
                    pe.wait_ge(s_qhi, j + 1)
                    pe.wait_ge(s_qlo, j + 1)
                    if i == 0:
                        wait(pe, s_evx, j - 3)
                    else:
                        pe.wait_ge(s_evh, 2 * j + 1)
                    for b in range(2):
                        for u in range(2):
                            hh = 2 * (2 * i + b)
                            mm = pe.transpose(
                                p_tr[:, b * NP + u * PT:b * NP + (u + 1) * PT],
                                q_hl[:, p, u * H + hh:u * H + hh + 2, :, :].rearrange("p h w d -> p (h w d)").bitcast(F32),
                                ident[0:PT, 0:PT])
                    mm.then_inc(s_trh, 1)

                def project(j, u):
                    if u == 0:
                        pe.wait_ge(s_y[0], j + 1)
                        pe.wait_ge(s_y[1], j + 1)
                        wait(pe, s_x2, j)
                    for g in range(G):
                        mm = pe.matmul(p_proj[0:PT, u * D:(u + 1) * D], y_t[:, g, u * PT:(u + 1) * PT], wproj[:, g, :],
                                       start=g == 0, stop=g == G - 1)
                    if u == 1:
                        mm.then_inc(s_proj, 1)

                def step(j, r, div):
                    p = r % 2
                    main, nxt, prev = (inside(j + d, TILES // 2) for d in (0, 1, -1))
                    for k in range(FILLS):
                        if main:
                            fill(j, p, k)
                        if prev:
                            if k == 0:
                                finish(1, j - 1, 1 - p)
                            if k == 2:
                                contract(1, j - 1, 2)
                                contract(1, j - 1, 3)
                            if k == 3:
                                spread_norm(1, j - 1, 1 - p)
                            if k in (9, 10):
                                project(j - 1, k // 10)
                        if nxt:
                            if k in (4, 7):
                                turn_hl(j + 1, 1 - p, k // 7)
                            if k == 11:
                                pe.wait_ge(s_qst, j + 2)
                                pe.wait_ge(s_evh, 2 * (j + 2))
                                for g in range(G):
                                    for u in range(2):
                                        mm = pe.transpose(p_tr[:, g * NP + u * PT:g * NP + (u + 1) * PT],
                                                          q_st[:, 1 - p, u * D + g * 128:u * D + (g + 1) * 128],
                                                          ident[0:PT, 0:PT])
                                mm.then_inc(s_trf, 1)
                        if main:
                            if k == 5:
                                contract(0, j, 0)
                                contract(0, j, 1)
                            if k == 8:
                                pe.wait_ge(s_evf, j + 1)
                                wait(pe, s_w2, 2 * j)
                                for g in range(G):
                                    mm = pe.matmul(p_gram[:, g * NP:(g + 1) * NP], gram[:, g, :], q_fT[:, p, g, :],
                                                   start=True, stop=True)
                                mm.then_inc(s_gram, 1)
                            if k == 11:
                                contract(0, j, 2)
                                contract(0, j, 3)
                            if k == 12:
                                finish(0, j, p)
                            if k == 13:
                                spread_norm(0, j, p)
                        if k == 0 and inside(j - 3, TILES // 2):
                            pe.wait_ge(s_xst, 2 * (j - 2))
                            wait(pe, s_gev, j - 3)
                            if isinstance(j, int):
                                wait(pe, s_evf, min(j + 1, TILES // 2))
                            for q in range(2):
                                for u in range(2):
                                    mm = pe.transpose(p_tr[:, q * NP + u * PT:q * NP + (u + 1) * PT],
                                                      x_st[:, 1 - p, u, q * 128:(q + 1) * 128], ident[0:PT, 0:PT])
                            mm.then_inc(s_trx, 1)
                        if k == 15:
                            gate_step(j, p, main)

                def gate_step(j, p, main):
                    a, b = gate_and_positions(j)
                    if a < b:
                        if isinstance(j, int):
                            wait(pe, s_evf, min(j + 2, TILES // 2))
                        else:
                            pe.wait_ge(s_evf, j + 2)
                    if a == 0:
                        pe.wait_ge(s_evx, j - 2)
                    for u in range(2):
                        if main:
                            contract(1, j, u)
                        if a == 0:
                            for q in range(2):
                                mm = pe.matmul(p_tr[0:PT, u * E:(u + 1) * E], x_T[:, q, u * PT:(u + 1) * PT],
                                               gate_t[:, q, :], start=q == 0, stop=q == 1)
                    if b == 4:
                        pe.wait_ge(s_oh, j - 3)
                        pe.matmul(p_tr[0:PT, 2 * E:4 * E], tri_b[:], one_hot[:, p, :, :].rearrange("p u e -> p (u e)"),
                                  start=True, stop=False)
                        mm = pe.matmul(p_tr[0:PT, 2 * E:4 * E], ones_b[:],
                                       before[:, p, :, :].rearrange("p u e -> p (u e)"), start=False, stop=True)
                    if a < b:
                        mm.then_inc(s_gate, 1)
                run(pe, -1, TILES // 2 + 4, step)

            @block.vector
            def _(dve):

                STEPS = 3

                def output(g, j, p):
                    dve.wait_ge(s_yn[g], j + 1)
                    wait(dve, s_proj, j)
                    dve.tensor_scalar(y_t[:, g, :], p_y[g][:, NP:2 * NP], float(N), None, ALU.add).then_inc(s_den[g], 1)
                    dve.wait_ge(s_den[g], j + 1)
                    dve.reciprocal(y_t[:, g, :], y_t[:, g, :]).then_inc(s_rden[g], 1)
                    dve.wait_ge(s_rden[g], j + 1)
                    c = 132 + 18 * g + ND
                    dve.scalar_tensor_tensor(out=y_t[:, g, :], in0=p_y[g][:, 0:NP], scalar=sums[:, c:c + 1],
                                             in1=y_t[:, g, :], op0=ALU.add, op1=ALU.mult).then_inc(s_y[g], 1)

                def step(j, r, div):
                    p = r % 2
                    if isinstance(j, int) and j == 3:
                        dve.wait_ge(b_ini, 7)
                        dve.wait_ge(b_ld, LOADS)
                    if inside(j - 2, TILES // 2):
                        dve.wait_ge(s_rs2, j - 1)
                        wait(dve, s_trx, j - 3)
                        for u in range(2):
                            a = row[:, (r - 2) % 4, u, :]
                            dve.tensor_scalar(x_st[:, p, u, :], a[:, 0:D], a[:, MEAN:MEAN + 1], a[:, RSTD:RSTD + 1],
                                              ALU.subtract, ALU.mult).then_inc(s_xst, 1)
                    if inside(j + 2, TILES // 2):
                        wait(dve, s_trf, j + 1)
                        wait(dve, s_qhi, j + 1)
                        wait(dve, s_qlo, j + 1)
                        dve.tensor_copy(q_st[:, p, :], q_all[:, bass.ds(j * 2 + 4, 2), :].rearrange("p t d -> p (t d)")
                                        ).then_inc(s_qst, 1)
                    if inside(j - 5, TILES // 2):
                        dve.wait_ge(s_gev, j - 3)
                        dve.tensor_tensor(pm[:], lg[:, 1 - p, 2:4, :], one_hot[:, 1 - p, :, :], ALU.mult
                                          ).then_inc(s_route, 1)
                        dve.wait_ge(s_route, STEPS * (j - 5) + 1)
                        dve.tensor_reduce(pos[:], pm[:], AX_X, ALU.add).then_inc(s_pos, 1)
                        dve.wait_ge(s_pos, j - 4)
                        dve.tensor_scalar(over[:], pos[:], float(CAP), NO_TOKEN, ALU.is_gt, ALU.mult).then_inc(s_route, 1)
                        dve.scalar_tensor_tensor(out=at[:], in0=rev_max[:, 1 - p, :], scalar=-float(SLOTS), in1=pos[:],
                                                 op0=ALU.mult, op1=ALU.add).then_inc(s_route, 1)
                        dve.wait_ge(s_route, STEPS * (j - 5) + 3)
                        wait(dve, s_scat[(r - 7) % 4], 32 * div(-3, 4))
                        dve.scalar_tensor_tensor(out=slot[:, 1 - p, :], in0=at[:], scalar=float(E * SLOTS - 1),
                                                 in1=over[:], op0=ALU.add, op1=ALU.add).then_inc(s_slot, 1)
                    if inside(j - 4, TILES // 2):
                        rev = cst[0:PT, C_REV:C_REV + E].unsqueeze(1).to_broadcast([PT, 2, E])
                        dve.wait_ge(s_gev, j - 3)
                        dve.tensor_tensor(lgb[:], lg[:, 1 - p, 0:2, :], gateb_t[:].unsqueeze(1).to_broadcast([PT, 2, E]),
                                          ALU.add).then_inc(s_lgb, 1)
                        dve.wait_ge(s_lgb, j - 3)
                        dve.tensor_reduce(rmax[:], lgb[:], AX_X, ALU.max).then_inc(s_rmax, 1)
                        dve.wait_ge(s_rmax, j - 3)
                        wait(dve, s_rex, j - 4)
                        dve.tensor_tensor(rd[:], lgb[:], rmax[:].unsqueeze(2).to_broadcast([PT, 2, E]),
                                          ALU.subtract).then_inc(s_rd, 1)
                        dve.wait_ge(s_rd, j - 3)
                        dve.scalar_tensor_tensor(out=rw[:], in0=rd[:], scalar=0.0, in1=rev, op0=ALU.is_equal,
                                                 op1=ALU.mult).then_inc(s_rw, 1)
                        dve.wait_ge(s_rw, j - 3)
                        dve.tensor_reduce(rev_max[:, p, :], rw[:], AX_X, ALU.max).then_inc(s_rev, 1)
                        dve.wait_ge(s_rev, j - 3)
                        dve.tensor_tensor(one_hot[:, p, :, :], rev, rev_max[:, p, :].unsqueeze(2).to_broadcast([PT, 2, E]),
                                          ALU.is_equal).then_inc(s_hot, 1)
                        dve.tensor_tensor(before[:, p, 0, :], before[:, 1 - p, 1, :], one_hot[:, 1 - p, 1, :],
                                          ALU.add).then_inc(s_hot, 1)
                        dve.wait_ge(s_hot, 2 * (j - 3))
                        dve.tensor_tensor(before[:, p, 1, :], before[:, p, 0, :], one_hot[:, p, 0, :],
                                          ALU.add).then_inc(s_oh, 1)
                    if inside(j, TILES // 2):
                        dve.wait_ge(s_g[p], 64 * (div(0, 2) + 1))
                        dve.tensor_tensor(ga[:], rows[:, p, :, D:TW], alr_g[:, p, :, GH:2 * GH], ALU.add).then_inc(s_ga, 1)
                        dve.wait_ge(s_ga, j + 1)
                        dve.scalar_tensor_tensor(out=gl[:], in0=ga[:], scalar=0.01, in1=ga[:], op0=ALU.mult,
                                                 op1=ALU.max).then_inc(s_gl, 1)
                        dve.wait_ge(s_gl, j + 1)
                        dve.tensor_reduce(gmax[:], gl[:], AX_X, ALU.max).then_inc(s_gmax, 1)
                        dve.wait_ge(s_gmax, j + 1)
                        wait(dve, s_ge, j)
                        dve.tensor_tensor(gs[:], gl[:], gmax[:].unsqueeze(2).to_broadcast([PT, 2, GH]),
                                          ALU.subtract).then_inc(s_gs, 1)
                    if inside(j - 1, TILES // 2):
                        output(1, j - 1, 1 - p)
                    if inside(j + 2, TILES // 2):
                        dve.wait_ge(s_qhi, j + 3)
                        wait(dve, s_trh, 2 * (j + 1))
                        dve.tensor_tensor(q_hl[:, p, :, 1, :], q_st[:, p, :].rearrange("p (h d) -> p h d", d=HD),
                                          q_hl[:, p, :, 0, :].bitcast(F32), ALU.subtract).then_inc(s_qlo, 1)
                    if inside(j, TILES // 2):
                        dve.wait_ge(s_ge, j + 1)
                        dve.tensor_reduce(gsum[:], ge[:], AX_X, ALU.add).then_inc(s_gsum, 1)
                        dve.wait_ge(s_gsum, j + 1)
                        dve.reciprocal(grec[:], gsum[:]).then_inc(s_grec, 1)
                        dve.wait_ge(s_grec, j + 1)
                        wait(dve, s_prod, j)
                        dve.tensor_tensor(gp[:], ge[:], grec[:].unsqueeze(2).to_broadcast([PT, 2, GH]),
                                          ALU.mult).then_inc(s_gp, 1)
                    if inside(j, TILES // 2):
                        dve.wait_ge(s_gram, j + 1)
                        wait(dve, s_wh, j)
                        wait(dve, s_wl, j)
                        for g in range(G):
                            dve.scalar_tensor_tensor(out=w_t[:, g, :], in0=p_gram[:, g * NP:(g + 1) * NP],
                                                     scalar=sums[:, 66 * g:66 * g + 1], in1=q_fT[:, p, g, :],
                                                     op0=ALU.add, op1=ALU.mult).then_inc(s_w2, 1)
                    if inside(j, TILES // 2):
                        dve.wait_ge(s_prod, j + 1)
                        wait(dve, s_gadd, j - 1)
                        dve.tensor_reduce(tmp[:, p, :, :], prod[:].rearrange("p t h d -> p t d h"), AX_X,
                                          ALU.add).then_inc(s_tmp, 1)
                    if inside(j - 1, TILES // 2):
                        dve.wait_ge(s_proj, j)
                        dve.wait_ge(s_gadd, j)
                        wait(dve, s_scat[(r - 1) % 4], 32 * div(-1, 4))
                        wait(dve, s_out[(r - 1) % 4], 16 * div(-1, 4))
                        dve.tensor_tensor(row[:, (r - 1) % 4, :, 0:D], p_proj[0:PT, :].rearrange("p (t d) -> p t d", t=2),
                                          x_all[:, bass.ds(j * 2 - 2, 2), :], ALU.add).then_inc(s_x2, 1)
                        dve.wait_ge(s_x2, j)
                        wait(dve, s_mv2, 2 * (j - 1))
                        dve.sem_inc(b_met[1], 1)
                        for u in range(2):
                            dve.bn_stats(st2[:, u, :], row[:, (r - 1) % 4, u, 0:D]).then_inc(s_st2, 1)
                        dve.wait_ge(s_st2, 2 * j)
                        dve.sem_inc(b_met[1], 1)
                        for u in range(2):
                            dve.bn_aggr(row[:, (r - 1) % 4, u, MEAN:VAR + 1], st2[:, u, :]).then_inc(s_mv2, 1)
                    if inside(j - 4, TILES // 2):
                        dve.wait_ge(s_rex, j - 3)
                        dve.tensor_reduce(rsum[:], rex[:], AX_X, ALU.add).then_inc(s_rsum, 1)
                        dve.tensor_scalar(row[:, (r - 4) % 4, :, TOKEN], cst[0:PT, bass.ds(j * 2 + (C_TOK - 8), 2)], 1.0,
                                          None, ALU.mult).then_inc(s_rsum, 1)
                        dve.wait_ge(s_rsum, 2 * (j - 3))
                        dve.reciprocal(row[:, (r - 4) % 4, :, GATE], rsum[:]).then_inc(s_gt, 1)
                    if inside(j, TILES // 2):
                        output(0, j, p)
                run(dve, -2, TILES // 2 + 5, step)


def first_views(q_full):
    return (q_full[:, 6:14, :].rearrange("p (k t) d -> p k (t d)", k=2), q_full[:, 14:22, :],
            q_full[0:E * FC, 30, 0:128], q_full[0:SP_, 22:30, :])


def load_first(sp, q_full, first, w1, b1, w2, b2):
    w1_raw, w2_raw, b1_rows, b2_all = first_views(q_full)
    sp.dma_start(w1_raw, w1[0].rearrange("(k p) f -> p k f", p=128)).then_inc(first["w1"], 16)
    sp.dma_start(w2_raw, w2[0].rearrange("(c p) d -> p c d", p=128)).then_inc(first["w2"], 16)
    sp.dma_start(b1_rows, b1.rearrange("e (c m) -> (e c) m", m=128)).then_inc(first["b"], 16)
    sp.dma_start(b2_all.rearrange("p e d -> p (e d)"),
                 b2.rearrange("e d -> (e d)").partition_broadcast(SP_)).then_inc(first["b"], 16)


def build_experts(nc, sem, scope, w1, w2, slots, out, ident, q_full, first):
    with scope:
        def sb(name, shape, dt=F32):
            return scope.enter_context(nc.sbuf_tensor(name, shape, dt))

        def ps(name):
            return scope.enter_context(nc.psum_tensor(name, [128, 512], F32))

        BI = SI // 2
        w1_raw, w2_raw, b1_rows, b2_all = first_views(q_full)
        w1_hi, w1_lo = sb("w1_hi", [128, 2, 2, F], F32R), sb("w1_lo", [128, 2, 2, F], F32R)
        w2_hi, w2_lo = sb("w2_hi", [128, 2, FC, D], F32R), sb("w2_lo", [128, 2, FC, D], F32R)
        b1_T, b1_now = sb("b1_T", [128, E * FC]), sb("b1_now", [128, 2, FC])
        rows = sb("slot_rows", [SP_, 4, BI, RW])
        token = sb("token", [SP_, 4, BI], I32)
        xn = sb("xn_e", [SP_, BI, D])
        xT_hi, xT_lo = sb("xTe_hi", [128, 2, 2, HALF], F32R), sb("xTe_lo", [128, 2, 2, HALF], F32R)
        h32 = sb("h32", [128, 4, HALF])
        h_hi, h_lo = sb("h_hi", [128, 4, HALF], F32R), sb("h_lo", [128, 4, HALF], F32R)
        yb, z, big, fin, alt = (q_full[0:SP_, n:n + 4, :].rearrange("p i d -> p (i d)") for n in (31, 35, 39, 43, 0))
        res = sb("res", [SP_, 2, BI, D])

        p_h = [ps("p_h0"), ps("p_h1")]
        p_x = [ps("p_x0"), ps("p_x1")]
        p_o = [[ps(f"p_o{b}{i}") for i in range(2)] for b in range(2)]

        e_b1t, e_b1 = sem("e_b1t"), sem("e_b1")
        e_met = [sem("e_met_pool"), sem("e_met_dve")]
        s_w1ld, s_w2ld, s_rows = first["w1"], first["w2"], [sem(f"e_rows{i}") for i in range(4)]
        s_whi, s_wlo, s_b1 = sem("e_whi"), sem("e_wlo"), sem("s_b1")
        s_xn, s_tok, s_tr, s_xhi, s_xlo = sem("e_xn"), sem("s_tok"), sem("s_tr"), sem("s_xhi"), sem("s_xlo")
        s_hmm, s_h32, s_hhi, s_hlo, s_ymm = sem("s_hmm"), sem("s_h32"), sem("s_hhi"), sem("s_hlo"), sem("s_ymm")
        s_yb, s_z, s_cmp, s_alt, s_alt2, s_sel, s_res = (
            sem(n) for n in ("s_yb", "s_z", "s_cmp", "s_alt", "s_alt2", "s_selz", "s_res"))
        s_put = [sem("s_put0"), sem("s_put1")]
        FLT_MAX = float(np.finfo(np.float32).max)
        PIECES = 2 * BI

        def run(eng, first, last, step):
            pipeline(eng, first, last, 2, 6, step)

        def part(a, q):
            return a[:, q * 2 * D:(q + 1) * 2 * D]

        def piece(w_1, w_2, c, *slot):
            a = w_1[(slice(None), *slot)] if slot else w_1[:]
            b = w_2[(slice(None), *slot)] if slot else w_2[:]
            a = a.rearrange("p k f -> p (k f)") if c < BI else b.rearrange("p c d -> p (c d)")
            return a[:, (c % BI) * 512:(c % BI) * 512 + 512]

        with nc.Block() as block:
            @block.sync
            def _(sp):
                def step(e, p, div):
                    if inside(e + 1, E):
                        ahead = not (isinstance(e, int) and e == -1)
                        if ahead:
                            wait(sp, s_wlo, PIECES * (e + 1))
                            sp.dma_start(w1_raw[:], w1[bass.ds(e + 1, 1), :, :].rearrange("o (k p) f -> p (o k) f", p=128)
                                         ).then_inc(s_w1ld, 16)
                        for b in range(2):
                            wait(sp, s_res, 2 * (2 * (e - 1) + b + 1))
                            wait(sp, s_tok, 2 * (e - 1) + b + 1)
                            sp.dma_start(rows[:, 2 * (1 - p) + b, :, :],
                                         slots[bass.ds(e * SLOTS + SLOTS, SLOTS), :]
                                         .rearrange("(p i) d -> p i d", i=SI)[:, b * BI:(b + 1) * BI, :]
                                         ).then_inc(s_rows[2 * (1 - p) + b], 16)
                        if ahead:
                            sp.dma_start(w2_raw[:], w2[bass.ds(e + 1, 1), :, :].rearrange("o (c p) d -> p (o c) d", p=128)
                                         ).then_inc(s_w2ld, 16)
                run(sp, -1, E, step)

            @block.gpsimd
            def _(pool):
                def step(e, p, div):
                    for b in range(2):
                        s = e * 2 + b
                        for c in range(FC):
                            k = e * 2 * FC + (b * FC + c)
                            if c == 1 and inside(s - 2, 2 * E):
                                for i in range(BI):
                                    pool.wait_ge(s_res, s * 2 + (i // 2 - 3))
                                    pool.sem_inc(e_met[0], 1)
                                    pool.indirect_dma_start(
                                        out, bass.IndirectOffsetOnAxis(ap=token[:, (2 * p + b - 2) % 4, i:i + 1], axis=0),
                                        res[:, b, i, :], None, bounds_check=N - 1, oob_is_err=False).then_inc(s_put[b], 16)
                run(pool, 0, E + 1, step)
                for b in range(2):
                    pool.wait_ge(s_put[b], 16 * BI * E)

            @block.scalar
            def _(act):
                act.wait_ge(e_b1t, 1)
                act.activation(b1_T[:], p_h[0][:, 0:E * FC], ACT.Copy).then_inc(e_b1, 1)

                def step(e, p, div):
                    for b in range(2):
                        s = e * 2 + b
                        for c in range(FC):
                            k = e * 2 * FC + (b * FC + c)
                            if inside(e, E):
                                if b == 0 and c == 0:
                                    act.wait_ge(s_b1, e + 1)
                                act.wait_ge(s_hmm, k + 1)
                                wait(act, s_hlo, k - 3)
                                act.activation(h32[:, c % 4, :], p_h[c % 2][:, 0:HALF], ACT.Relu,
                                               bias=b1_now[:, p, c:c + 1]).then_inc(s_h32, 1)
                                act.wait_ge(s_h32, k + 1)
                                wait(act, s_ymm, k - 3)
                                act.activation(h_hi[:, c % 4, :], h32[:, c % 4, :], ACT.Copy).then_inc(s_hhi, 1)
                            if c == 6 and inside(s - 1, 2 * E):
                                for q in range(2):
                                    act.wait_ge(s_alt, s * 2 + (q - 1))
                                    act.activation(part(alt, q), part(alt, q), ACT.Copy, scale=-10000.0
                                                   ).then_inc(s_alt2, 1)
                            if c in (4, 5) and inside(s + 1, 2 * E):
                                act.wait_ge(s_tr, 2 * (s + 1) + c - 3)
                                wait(act, s_hmm, FC * s)
                                act.activation(xT_hi[:, 1 - b, c - 4, :], p_x[c - 4][:, 0:HALF],
                                               ACT.Copy).then_inc(s_xhi, 1)
                            if b == 1 and inside(e + 1, E):
                                if c == 0:
                                    act.wait_ge(s_w1ld, 16 * (e + 2))
                                    wait(act, s_hmm, 2 * FC * e)
                                if c == BI:
                                    act.wait_ge(s_w2ld, 16 * (e + 2))
                                    wait(act, s_ymm, 2 * FC * e)
                                act.activation(piece(w1_hi, w2_hi, c, 1 - p), piece(w1_raw, w2_raw, c),
                                               ACT.Copy).then_inc(s_whi, 1)
                            if c == 2 and inside(s - 1, 2 * E):
                                act.wait_ge(s_yb, 2 * s)
                                wait(act, s_sel, 2 * (s - 1))
                                for i in range(BI):
                                    act.activation(z[:, i * D:(i + 1) * D], yb[:, i * D:(i + 1) * D], ACT.Copy,
                                                   scale=rows[:, (2 * p + b - 1) % 4, i, GATE:GATE + 1]).then_inc(s_z, 1)
                run(act, -1, E + 1, step)

            @block.tensor
            def _(pe):
                pe.wait_ge(first["b"], 32)
                pe.transpose(p_h[0][:, 0:E * FC], b1_rows, ident[0:E * FC, 0:E * FC]).then_inc(e_b1t, 1)
                pe.wait_ge(e_b1, 1)

                def step(e, p, div):
                    for b in range(2):
                        s = e * 2 + b
                        for c in range(FC):
                            k = e * 2 * FC + (b * FC + c)
                            if inside(e, E):
                                if c == 0:
                                    pe.wait_ge(s_xlo, 2 * (s + 1))
                                    if b == 0:
                                        pe.wait_ge(s_wlo, PIECES * e + BI)
                                wait(pe, s_h32, k - 1)
                                n = 0
                                for kk in range(2):
                                    for w, x in ((w1_hi, xT_hi), (w1_hi, xT_lo), (w1_lo, xT_hi)):
                                        mm = pe.matmul(p_h[c % 2][:, 0:HALF], w[:, p, kk, c * 128:(c + 1) * 128],
                                                       x[:, b, kk, :], start=n == 0, stop=n == 5)
                                        n += 1
                                mm.then_inc(s_hmm, 1)
                            if c in (3, 4) and inside(s + 1, 2 * E):
                                pe.wait_ge(s_xn, BI * (s + 2))
                                wait(pe, s_xlo, 2 * (s + 1))
                                for i in range(BI):
                                    mm = pe.transpose(p_x[c - 3][:, i * SP_:(i + 1) * SP_],
                                                      xn[:, i, (c - 3) * 128:(c - 2) * 128], ident[0:SP_, 0:SP_])
                                mm.then_inc(s_tr, 1)
                            late = c < 2
                            if inside(s - 1, 2 * E) if late else inside(e, E):
                                cy, by = (c - 2) % FC, 1 - b if late else b
                                py = 1 - p if late and b == 0 else p
                                pe.wait_ge(s_hlo, k - 1)
                                if cy == 0 and by == 0:
                                    pe.wait_ge(s_wlo, PIECES * (e + 1))
                                if cy == 0:
                                    wait(pe, s_yb, 2 * (s - 1))
                                for i in range(BI):
                                    n = 0
                                    for a, w in ((h_hi, w2_hi), (h_hi, w2_lo), (h_lo, w2_hi)):
                                        mm = pe.matmul(p_o[by][i // 2][0:SP_, (i % 2) * D:(i % 2 + 1) * D],
                                                       a[:, cy % 4, i * SP_:(i + 1) * SP_], w[:, py, cy, :],
                                                       start=cy == 0 and n == 0 and i % 2 == 0,
                                                       stop=cy == FC - 1 and n == 2, skip_group_check=True)
                                        n += 1
                                mm.then_inc(s_ymm, 1)
                run(pe, -1, E + 1, step)

            @block.vector
            def _(dve):
                dve.wait_ge(first["b"], 32)
                dve.wait_ge(e_b1, 1)

                def step(e, p, div):
                    for b in range(2):
                        s = e * 2 + b
                        for c in range(FC):
                            k = e * 2 * FC + (b * FC + c)
                            if inside(e, E):
                                dve.wait_ge(s_hhi, k + 1)
                                wait(dve, s_ymm, k - 3)
                                dve.tensor_tensor(h_lo[:, c % 4, :], h32[:, c % 4, :], h_hi[:, c % 4, :].bitcast(F32),
                                                  ALU.subtract).then_inc(s_hlo, 1)
                            if c == 1 and inside(s + 1, 2 * E):
                                to = (2 * p + b + 1) % 4
                                dve.wait_ge(s_rows[to], 16 * (div(b, 2) + 1))
                                wait(dve, s_tr, 2 * (s + 1))
                                for i in range(BI):
                                    a = rows[:, to, i, :]
                                    dve.tensor_scalar(xn[:, i, :], a[:, 0:D], a[:, MEAN:MEAN + 1], a[:, RSTD:RSTD + 1],
                                                      ALU.subtract, ALU.mult).then_inc(s_xn, 1)
                                wait(dve, s_put[1 - b], 16 * BI * (e - 1 + b))
                                dve.tensor_copy(token[:, to, :], rows[:, to, :, TOKEN]).then_inc(s_tok, 1)
                            if c in (4, 5) and inside(s + 1, 2 * E):
                                dve.wait_ge(s_xhi, 2 * (s + 1) + c - 3)
                                dve.tensor_tensor(xT_lo[:, 1 - b, c - 4, :], p_x[c - 4][:, 0:HALF],
                                                  xT_hi[:, 1 - b, c - 4, :].bitcast(F32), ALU.subtract).then_inc(s_xlo, 1)
                            if b == 1 and inside(e + 1, E):
                                dve.wait_ge(s_whi, PIECES * (e + 1) + c + 1)
                                dve.tensor_tensor(piece(w1_lo, w2_lo, c, 1 - p), piece(w1_raw, w2_raw, c),
                                                  piece(w1_hi, w2_hi, c, 1 - p).bitcast(F32),
                                                  ALU.subtract).then_inc(s_wlo, 1)
                                if c == 7:
                                    wait(dve, s_h32, 2 * FC * e)
                                    dve.tensor_scalar(b1_now[:, 1 - p, :], b1_T[:, bass.ds(e * FC + FC, FC)], 1.0, None,
                                                      ALU.mult).then_inc(s_b1, 1)
                            if c == 1 and inside(s - 1, 2 * E):
                                dve.wait_ge(s_ymm, FC * s)
                                wait(dve, s_z, BI * (s - 1))
                                for i in range(2):
                                    dve.tensor_tensor(
                                        yb[:, i * 2 * D:(i + 1) * 2 * D].rearrange("p (i d) -> p i d", i=2),
                                        p_o[1 - b][i][0:SP_, :].rearrange("p (i d) -> p i d", i=2),
                                        b2_all[:, bass.ds(e + (b - 1), 1), :].to_broadcast([SP_, 2, D]),
                                        ALU.add).then_inc(s_yb, 1)
                            if c == 3 and inside(s - 1, 2 * E):
                                for q in range(2):
                                    dve.wait_ge(s_z, s * BI + (2 * q - 2))
                                    wait(dve, s_alt, 2 * (s - 1))
                                    dve.tensor_scalar(part(big, q), part(z, q), FLT_MAX, None, ALU.is_gt).then_inc(s_cmp, 1)
                                    dve.tensor_scalar(part(fin, q), part(z, q), 0.0, 0.0, ALU.mult, ALU.is_equal
                                                      ).then_inc(s_cmp, 1)
                                    dve.wait_ge(s_cmp, s * 4 + (2 * q - 2))
                                    wait(dve, s_res, 2 * (s - 1))
                                    dve.scalar_tensor_tensor(out=part(alt, q), in0=part(z, q), scalar=-FLT_MAX,
                                                             in1=part(big, q), op0=ALU.is_lt, op1=ALU.subtract
                                                             ).then_inc(s_alt, 1)
                            if c == 7 and inside(s - 1, 2 * E):
                                for q in range(2):
                                    dve.wait_ge(s_alt2, s * 2 + (q - 1))
                                    dve.sem_inc(e_met[1], 1)
                                    dve.copy_predicated(part(alt, q), part(fin, q).bitcast(U32), part(z, q)
                                                        ).then_inc(s_sel, 1)
                                for q in range(2):
                                    dve.wait_ge(s_sel, s * 2 + (q - 1))
                                    wait(dve, s_put[1 - b], 16 * BI * (e - 1 + b))
                                    dve.tensor_tensor(res[:, 1 - b, 2 * q:2 * q + 2, :],
                                                      rows[:, (2 * p + b - 1) % 4, 2 * q:2 * q + 2, 0:D],
                                                      part(alt, q).rearrange("p (i d) -> p i d", i=2), ALU.add
                                                      ).then_inc(s_res, 1)
                run(dve, -1, E + 1, step)



_INS = ["x", "src", "dst", "wg", "attn_l", "attn_r", "wqkvT", "bqkv", "wprojT", "bproj", "temp", "gate_w", "gate_b",
        "w1", "b1", "w2", "b2", "consts", "pair_sel"]


def kernel(**inp):
    import concourse.bacc as bacc
    from concourse.bass_utils import run_bass_kernel_spmd as launch

    c = np.ascontiguousarray
    arrays = {
        "x": c(inp["x"]), "src": c(inp["src"][:N]), "dst": c(inp["dst"][:N]),
        "wg": c(inp["L0_gnn_weight"]), "attn_l": c(inp["L0_gnn_attn_l"]).reshape(-1),
        "attn_r": c(inp["L0_gnn_attn_r"]).reshape(-1), "wqkvT": c(inp["L0_mix_Wqkv"].T),
        "bqkv": c(inp["L0_mix_bqkv"]), "wprojT": c(inp["L0_mix_Wproj"].T), "bproj": c(inp["L0_mix_bproj"]),
        "temp": c(inp["L0_mix_temperature"]).reshape(-1), "gate_w": c(inp["L0_ffn_gate_w"]),
        "gate_b": c(inp["L0_ffn_gate_b"]), "w1": c(inp["L0_ffn_w1"]), "b1": c(inp["L0_ffn_b1"]),
        "w2": c(inp["L0_ffn_w2"]), "b2": c(inp["L0_ffn_b2"]), "consts": constants(), "pair_sel": selections(),
    }
    nc = bacc.Bacc("TRN2", target_bir_lowering=False, num_devices=1)
    args = [nc.dram_tensor("in_" + k, arrays[k].shape, mybir.dt.from_np(arrays[k].dtype), kind="ExternalInput").ap()
            for k in _INS]
    out = nc.dram_tensor("out", (N, D), F32, kind="ExternalOutput").ap()
    table = nc.dram_tensor("table", (N, TW), F32, kind="Internal").ap()
    alr_table = nc.dram_tensor("alr_table", (N, 2 * GH), F32, kind="Internal").ap()
    slots = nc.dram_tensor("slots", (E * SLOTS, RW), F32, kind="Internal").ap()
    build(nc, *args, out, table, alr_table, slots)
    r = launch(nc, [{"in_" + k: v for k, v in arrays.items()}], core_ids=[0])
    return r.results[0]["out"]
```
